# Optimizing a Trainium2 kernel written in Bass

```python
import numpy as np
import jax
import jax.numpy as jnp

def _softmax(x, axis=-1):
    return jax.nn.softmax(x, axis=axis)

def _gelu(x):
    return jax.nn.gelu(x, approximate=True)

def _silu(x):
    return jax.nn.silu(x)

def _sigmoid(x):
    return jax.nn.sigmoid(x)

def _layernorm(x, axis=-1, eps=1e-05):
    m = jnp.mean(x, axis=axis, keepdims=True)
    v = jnp.var(x, axis=axis, keepdims=True)
    return (x - m) / jnp.sqrt(v + eps)

def _scatter_add(tgt, idx, src, axis=0):
    return tgt.at[idx].add(src)

def _segment_sum(src, seg, n):
    return jax.ops.segment_sum(src, seg, n)
kernel_name = 'mk_xattn_ffn_d1_seqx_r4_385b17'

def setup_inputs(seed: int=0):
    np.random.seed(seed)
    _w = jnp.asarray

    def _rec_inputs():
        import jax
        import jax.numpy as jnp
        _rk = jax.random.key(seed)
        x = -0.000125 + 0.9999 * jax.random.normal(jax.random.fold_in(_rk, 1), (8, 256, 256), jnp.float32)
        _lenS = 256 - jax.random.randint(jax.random.fold_in(_rk, 7), (8,), 0, max(1, 256 // 4) + 1, jnp.int32)
        _lenS2 = 256 - jax.random.randint(jax.random.fold_in(_rk, 8), (8,), 0, max(1, 256 // 4) + 1, jnp.int32)
        _ctx_1024P = jax.random.normal(jax.random.fold_in(_rk, 11), (8, 16, 256), jnp.float32)
        _ctx_1024c = jax.random.dirichlet(jax.random.fold_in(_rk, 511), 0.3 * jnp.ones((16,), jnp.float32), (8, 256))
        _ctx_1024t = jnp.einsum('bsk,bkd->bsd', _ctx_1024c, _ctx_1024P)
        _ctx_1024t = _ctx_1024t * jax.lax.rsqrt(jnp.mean(jnp.square(_ctx_1024t)) + 1e-12) * 0.953939
        ctx_1024 = -1.52775e-05 + 0.999936 * (_ctx_1024t + 0.3 * jax.random.normal(jax.random.fold_in(_rk, 611), (8, 256, 256), jnp.float32))
        return (x, ctx_1024)
    x, ctx_1024 = _rec_inputs()

    def _L0_xattn_setup():
        import jax, jax.numpy as jnp
        import numpy as np
        D_MODEL = 256
        HEAD_SIZE = 256
        CONTEXT_SIZE = 128
        key = jax.random.key(seed)
        kq, kk, kv, kwq, kwk, kwv = jax.random.split(key, 6)
        B, S = (64, 128)
        scale = 1.0 / np.sqrt(D_MODEL)
        return {'query': jax.random.normal(kq, (B, S, D_MODEL), dtype=jnp.float32), 'key': jax.random.normal(kk, (B, S, D_MODEL), dtype=jnp.float32), 'value': jax.random.normal(kv, (B, S, D_MODEL), dtype=jnp.float32), 'w_q': jax.random.normal(kwq, (D_MODEL, HEAD_SIZE), dtype=jnp.float32) * scale, 'w_k': jax.random.normal(kwk, (D_MODEL, HEAD_SIZE), dtype=jnp.float32) * scale, 'w_v': jax.random.normal(kwv, (D_MODEL, HEAD_SIZE), dtype=jnp.float32) * scale, 'mask': 1}
    _L0_xattn_all = _L0_xattn_setup()
    _L0_xattn_in = {k: v for k, v in _L0_xattn_all.items() if k in ('w_q', 'w_k', 'w_v')}
    del _L0_xattn_all

    def _L0_ffn_setup():
        import jax, jax.numpy as jnp
        import numpy as np
        B, T, D, R, E = (32, 256, 256, 64, 8)
        key = jax.random.key(seed)
        ks = jax.random.split(key, 12)
        inp = {}
        inp['x'] = jax.random.normal(ks[0], (B, T, D), dtype=jnp.float32)
        inp['base_W'] = jax.random.normal(ks[1], (D, D), dtype=jnp.float32) * (1.0 / np.sqrt(D))
        inp['base_b'] = jax.random.normal(ks[2], (D,), dtype=jnp.float32) * 0.01
        inp['disc_mu'] = jax.random.normal(ks[3], (E, D), dtype=jnp.float32) * 0.5
        inp['disc_sigma'] = jax.random.uniform(ks[4], (E, D), dtype=jnp.float32, minval=0.5, maxval=1.5)
        inp['down_W'] = jax.random.normal(ks[5], (E, D, R), dtype=jnp.float32) * (1.0 / np.sqrt(D))
        inp['down_b'] = jax.random.normal(ks[6], (E, R), dtype=jnp.float32) * 0.01
        inp['up_W'] = jax.random.normal(ks[7], (E, R, D), dtype=jnp.float32) * (1.0 / np.sqrt(R))
        inp['up_b'] = jax.random.normal(ks[8], (E, D), dtype=jnp.float32) * 0.01
        inp['conv_W'] = jax.random.normal(ks[9], (E, D, D), dtype=jnp.float32) * 0.02
        inp['conv_b'] = jax.random.normal(ks[10], (E, D), dtype=jnp.float32) * 0.01
        return inp
    _L0_ffn_all = _L0_ffn_setup()
    _L0_ffn_in = {k: v for k, v in _L0_ffn_all.items() if k in ('base_W', 'base_b', 'disc_mu', 'disc_sigma', 'down_W', 'down_b', 'up_W', 'up_b', 'conv_W', 'conv_b')}
    del _L0_ffn_all
    return {'x': x, 'ctx_1024': ctx_1024, 'L0_xattn_w_q': _L0_xattn_in['w_q'], 'L0_xattn_w_k': _L0_xattn_in['w_k'], 'L0_xattn_w_v': _L0_xattn_in['w_v'], 'L0_ffn_base_W': _L0_ffn_in['base_W'], 'L0_ffn_base_b': _L0_ffn_in['base_b'], 'L0_ffn_disc_mu': _L0_ffn_in['disc_mu'], 'L0_ffn_disc_sigma': _L0_ffn_in['disc_sigma'], 'L0_ffn_down_W': _L0_ffn_in['down_W'], 'L0_ffn_down_b': _L0_ffn_in['down_b'], 'L0_ffn_up_W': _L0_ffn_in['up_W'], 'L0_ffn_up_b': _L0_ffn_in['up_b'], 'L0_ffn_conv_W': _L0_ffn_in['conv_W'], 'L0_ffn_conv_b': _L0_ffn_in['conv_b']}

def reference(x, ctx_1024, L0_xattn_w_q, L0_xattn_w_k, L0_xattn_w_v, L0_ffn_base_W, L0_ffn_base_b, L0_ffn_disc_mu, L0_ffn_disc_sigma, L0_ffn_down_W, L0_ffn_down_b, L0_ffn_up_W, L0_ffn_up_b, L0_ffn_conv_W, L0_ffn_conv_b):
    import jax
    import jax.numpy as jnp

    def _L0_xattn_ref(query, key, value, w_q, w_k, w_v, mask):
        import jax, jax.numpy as jnp
        import numpy as np
        D_MODEL = 256
        HEAD_SIZE = 256
        CONTEXT_SIZE = 128
        q = jnp.einsum('bsd,dh->bsh', query, w_q)
        k = jnp.einsum('bsd,dh->bsh', key, w_k)
        v = jnp.einsum('bsd,dh->bsh', value, w_v)
        scale = 1.0 / np.sqrt(query.shape[-1]).astype(np.float32)
        scores = jnp.einsum('bqh,bkh->bqk', q, k) * scale
        if mask:
            S = scores.shape[1]
            causal = jnp.tril(jnp.ones((S, S), dtype=bool))
            scores = jnp.where(causal, scores, -jnp.inf)
        attn = jax.nn.softmax(scores, axis=-1)
        out = jnp.einsum('bqk,bkh->bqh', attn, v)
        return out

    def _L0_ffn_ref(x, base_W, base_b, disc_mu, disc_sigma, down_W, down_b, up_W, up_b, conv_W, conv_b):
        import jax, jax.numpy as jnp
        import numpy as np
        B, T, D, R, E = (32, 256, 256, 64, 8)
        base = jnp.einsum('btd,od->bto', x, base_W) + base_b
        m1 = x.mean(axis=1)
        m2 = (x * x).mean(axis=1)
        inv_var = 1.0 / (disc_sigma * disc_sigma)
        losses = (jnp.einsum('bd,ed->eb', m2, inv_var) - 2.0 * jnp.einsum('bd,ed->eb', m1, disc_mu * inv_var) + jnp.sum(disc_mu * disc_mu * inv_var, axis=1)[:, None]) / D
        idx = jnp.argmin(losses, axis=0)
        Wd, bd = (down_W[idx], down_b[idx])
        Wu, bu = (up_W[idx], up_b[idx])
        Wc, bc = (conv_W[idx], conv_b[idx])
        h = jax.nn.relu(jnp.einsum('btd,bdr->btr', x, Wd) + bd[:, None, :])
        a = jnp.einsum('btr,brd->btd', h, Wu) + bu[:, None, :]
        y = jnp.einsum('btd,bod->bto', a, Wc) + bc[:, None, :]
        return base + y
    x = x + _L0_xattn_ref(_layernorm(x, axis=-1), ctx_1024, ctx_1024, L0_xattn_w_q, L0_xattn_w_k, L0_xattn_w_v, 1)
    x = x + _L0_ffn_ref(_layernorm(x, axis=-1), L0_ffn_base_W, L0_ffn_base_b, L0_ffn_disc_mu, L0_ffn_disc_sigma, L0_ffn_down_W, L0_ffn_down_b, L0_ffn_up_W, L0_ffn_up_b, L0_ffn_conv_W, L0_ffn_conv_b)
    return x

_drawn_inputs = setup_inputs


def setup_inputs(seed=0):
    import zlib

    import numpy as np

    out = dict(_drawn_inputs(seed))
    spreads = {}
    factors = {'L0_ffn_base_b': 8.0, 'L0_ffn_down_b': 43.142, 'L0_ffn_up_b': 30.38, 'L0_ffn_conv_b': 8.0}
    for name, (base, spread) in spreads.items():
        noise = np.random.default_rng([zlib.crc32(name.encode()), seed]).standard_normal(out[name].shape)
        drawn = base * np.exp(spread * noise) if base else spread * noise
        out[name] = jnp.asarray(drawn.astype(out[name].dtype))
    for name, factor in factors.items():
        out[name] = (out[name] * factor).astype(out[name].dtype)
    return out
```

```python
import numpy as np
import concourse.bass as bass
from concourse import mybir
from contextlib import ExitStack


def xattn_ffn_program(nc, x, xT, ctxT, wqT, wkT, wv, base_wT, mu_T, sigma_T,
                      down_w, down_bT, up_aug, conv_wT, conv_b, base_b, out):
    f32 = mybir.dt.float32
    f32r = mybir.dt.float32r
    bf16 = mybir.dt.bfloat16
    u32 = mybir.dt.uint32
    ALU = mybir.AluOpType
    ACT = mybir.ActivationFunctionType
    AX = mybir.AxisListType

    P = 128
    B, S, D = x.shape
    E, R = down_w.shape[0], down_w.shape[2]
    KD = D // P
    QT = S // P
    SC = P * (1 + 2)
    EPS = 1e-5
    MASKED = -1e30
    HI, LO = 0, 1

    ctx = ExitStack()
    with ctx:
        def sb(name, shape, dt=f32):
            return ctx.enter_context(nc.sbuf_tensor(name, shape, dt))

        def pb(name, shape=(P, 512)):
            return ctx.enter_context(nc.psum_tensor(name, list(shape), f32))

        def sem(name):
            return ctx.enter_context(nc.semaphore(name))

        x_sb = sb("x_sb", [P, B, QT, D])
        xT_sb = sb("xT_sb", [P, B, KD, S])
        cT_sb = sb("cT_sb", [P, B, KD, S])
        wqT_sb = sb("wqT_sb", [P, KD, D])
        wkT_sb = sb("wkT_sb", [P, KD, D])
        wv_sb = sb("wv_sb", [P, KD, D])
        wb_sb = sb("wb_sb", [P, KD, D])
        mu_sb = sb("mu_sb", [P, KD, E])
        sg_sb = sb("sg_sb", [P, KD, E])
        dw_sb = sb("dw_sb", [P, E, KD, R])
        up_sb = sb("up_sb", [P, E, KD, P])
        cw_sb = sb("cw_sb", [P, E, KD, D])
        row_bias = sb("row_bias", [P, E, D])
        base_row = sb("base_row", [P, D])
        bd_aug = sb("bd_aug", [P, E])
        ident = sb("ident", [P, P])
        ident_h = sb("ident_h", [P, P], bf16)
        mask_h = sb("mask_h", [P, P], bf16)
        half_neg = sb("half_neg", [P, QT])
        ones_col = sb("ones_col", [P, 1])
        wq_sum = sb("wq_sum", [P, KD])
        wqc = sb("wqc", [P, KD, D])
        mc = [sb(f"mc{h}", [P, KD, D], f32r) for h in (HI, LO)]
        wvs = [sb(f"wvs{h}", [P, KD, D], f32r) for h in (HI, LO)]
        wbs = [sb(f"wbs{h}", [P, KD, D], f32r) for h in (HI, LO)]
        dws = sb("dws", [P, E, 2, KD, R], f32r)
        u_f = sb("u_f", [P, 2, D])
        us = sb("us", [P, E, 2, D], f32r)
        sg2 = sb("sg2", [P, KD, E])
        inv_var = sb("inv_var", [P, KD, E])
        mu_iv = sb("mu_iv", [P, KD, E])
        tab_m1 = sb("tab_m1", [P, KD, E])
        tab_m2 = sb("tab_m2", [P, KD, E])
        tab_c = sb("tab_c", [P, KD, E])
        loss_c = sb("loss_c", [1, E])
        xs = sb("xs", [P, 2, 2, KD, S], f32r)
        cs = sb("cs", [P, 2, 2, KD, S], f32r)
        ts = sb("ts", [P, 2, KD, S], f32r)
        vs = sb("vs", [P, 2, 2, QT, D], f32r)
        prob = sb("prob", [P, SC])
        pts = sb("pts", [P, 2, SC], f32r)
        stats1 = sb("stats1", [P, 2, QT, 6])
        mom1 = sb("mom1", [P, B, QT, 2])
        var1 = sb("var1", [P, QT])
        rs1 = sb("rs1", [P, B, QT])
        rmax = sb("rmax", [P, B, QT])
        nmax = sb("nmax", [P, B, QT])
        rsum = sb("rsum", [P, B, QT])
        rinv = sb("rinv", [P, B, QT])
        x2 = sb("x2", [P, B, QT, D])
        stats2 = sb("stats2", [P, 2, QT, 6])
        mom2 = sb("mom2", [P, B, QT, 2])
        var2 = sb("var2", [P, QT])
        rs2 = sb("rs2", [P, B, QT])
        z = sb("z", [P, QT, D])
        zs = sb("zs", [P, 2, 2, KD, S], f32r)
        sq = sb("sq", [P, S])
        pooled = sb("pooled", [P, B, 2 * KD])
        nloss = sb("nloss", [1, B, E])
        best = sb("best", [1, B, 8])
        pick = sb("pick", [1, B, 8], u32)
        dsel = sb("dsel", [P, 2, KD, P], f32r)
        bsel = sb("bsel", [P, 1])
        usel = sb("usel", [P, 2, D], f32r)
        h_f = sb("h_f", [P, S])
        hs = sb("hs", [P, 2, S], f32r)

        ps_t, ps_v, ps_s, ps_o, ps_z, ps_h = [pb(n) for n in ("ps_t", "ps_v", "ps_s", "ps_o", "ps_z", "ps_h")]
        ps_y = [pb("ps_y0"), pb("ps_y1")]
        t_ps = ps_t[:, :].rearrange("p (k s) -> p k s", k=KD)
        v_ps = ps_v[:, :].rearrange("p (k s) -> p k s", k=QT)
        o_ps = ps_o[:, :].rearrange("p (t d) -> p t d", t=QT)
        z_ps = ps_z[:, :].rearrange("p (k s) -> p k s", k=KD)
        h_ps = ps_h[:, 0:S]
        l_ps = ps_h[0:1, S:S + E]
        y_ps = [t[:, :].rearrange("p (t d) -> p t d", t=QT) for t in ps_y]

        wq_in, wk_in, wv_in, wb_in = sem("wq_in"), sem("wk_in"), sem("wv_in"), sem("wb_in")
        disc_in, down_in, bias_in = sem("disc_in"), sem("down_in"), sem("bias_in")
        up_in = [sem(f"up_in{j}") for j in range(2)]
        conv_in = [sem(f"conv_in{j}") for j in range(4)]
        xT_in = [sem(f"xT_in{b}") for b in range(B)]
        cT_in = [sem(f"cT_in{b}") for b in range(B)]
        x_in = [sem(f"x_in{b}") for b in range(B)]
        stored = sem("stored")
        names = ("id0 id_ok idh0 idh_ok mask0 mask_ok pow_ok ones_ok dpad_ok upad_ok bd0 bd_ok bias0 bias_ok "
                 "wq_summed wq_meaned wqc_ok mc_ready mc_hi mc_lo wv_hi wv_lo wb_hi wb_lo dw_hi dw_lo "
                 "sg2_ok iv_ok muiv_ok tab_ok lossc_ready lossc_ok u_ready u_sum u_hi u_lo "
                 "x_hi x_lo c_hi c_lo t_ready t_hi t_lo v_ready v_hi v_lo st1_ok mom1_ok var1_ok rs1_ok "
                 "s_ready max_ok nmax_ok exp_ok pt_ready pt_hi pt_lo o_ready rinv_ok x2_ok st2_ok mom2_ok "
                 "var2_ok rs2_ok z_ok z_ready z_hi z_sq z_lo l_ready nloss_ok best_ok pick_ok dsel_ok bsel_ok "
                 "usel_ok h_ready relu_ok h_hi h_lo base_ready y_ready fin_ok").split()
        q = {n: sem(n) for n in names}

        def raw(ap):
            return ap.bitcast(f32)

        block = ctx.enter_context(nc.Block())

        @block.sync
        def _(sp):
            def weights(dst, src, done):
                sp.dma_start(dst[:, :, :], src.rearrange("(k p) n -> p k n", p=P)).then_inc(done, 16)

            def transposed(dst, src, b, done):
                sp.dma_start(dst[:, b, :, :], src[b].rearrange("(k p) s -> p k s", p=P)).then_inc(done[b], 16)

            def batch(b):
                transposed(xT_sb, xT, b, xT_in)
                transposed(cT_sb, ctxT, b, cT_in)
                sp.dma_start(x_sb[:, b, :, :], x[b].rearrange("(t p) d -> p t d", p=P)).then_inc(x_in[b], 16)

            weights(wqT_sb, wqT, wq_in)
            weights(wkT_sb, wkT, wk_in)
            transposed(xT_sb, xT, 0, xT_in)
            transposed(cT_sb, ctxT, 0, cT_in)
            sp.dma_start(x_sb[:, 0, :, :], x[0].rearrange("(t p) d -> p t d", p=P)).then_inc(x_in[0], 16)
            weights(wv_sb, wv, wv_in)
            batch(1)
            sp.wait_ge(q["upad_ok"], 1)
            for j in range(4):
                if j % 2 == 0:
                    for e in range(4 * (j // 2), 4 * (j // 2) + 4):
                        sp.dma_start(up_sb[:, e, :, 0:R + 1],
                                     up_aug[e].rearrange("(k p) r -> p k r", p=P)).then_inc(up_in[j // 2], 16)
                for e in (2 * j, 2 * j + 1):
                    sp.dma_start(cw_sb[:, e, :, :],
                                 conv_wT[e].rearrange("(k p) o -> p k o", p=P)).then_inc(conv_in[j], 16)
                if j == 0:
                    sp.wait_ge(q["bias0"], 1)
                    sp.dma_start(row_bias[R:R + 1, :, :], conv_b.rearrange("(a e) d -> a e d", a=1)).then_inc(bias_in, 16)
                    sp.dma_start(base_row[R:R + 1, :], base_b.rearrange("(a d) -> a d", a=1)).then_inc(bias_in, 16)
                    weights(wb_sb, base_wT, wb_in)
                    sp.dma_start(mu_sb[:, :, :], mu_T.rearrange("(k p) e -> p k e", p=P)).then_inc(disc_in, 16)
                    sp.dma_start(sg_sb[:, :, :], sigma_T.rearrange("(k p) e -> p k e", p=P)).then_inc(disc_in, 16)
                if j == 1:
                    batch(2)
                    for e in range(E):
                        sp.dma_start(dw_sb[:, e, :, :],
                                     down_w[e].rearrange("(k p) r -> p k r", p=P)).then_inc(down_in, 16)
                    sp.wait_ge(q["bd0"], 2)
                    sp.dma_start(bd_aug[0:R, :], down_bT).then_inc(q["bd_ok"], 16)
            for b in range(3, B):
                batch(b)
            for b in range(B):
                sp.wait_ge(q["fin_ok"], b + 1)
                sp.dma_start(out[b].rearrange("(t p) d -> p t d", p=P), x2[:, b, :, :]).then_inc(stored, 16)
            sp.wait_ge(stored, 16 * B)

        @block.gpsimd
        def _(pool):
            g = nc.gpsimd

            def split(src, hi, lo, hi_done, lo_done, k):
                g.tensor_copy(hi, src).then_inc(hi_done, 1)
                pool.wait_ge(hi_done, k + 1)
                g.tensor_tensor(lo, src, raw(hi), ALU.subtract).then_inc(lo_done, 1)

            def split_x(b):
                pool.wait_ge(xT_in[b], 16)
                if b >= 2:
                    pool.wait_ge(q["t_ready"], b - 1)
                split(xT_sb[:, b, :, :], xs[:, b % 2, HI, :, :], xs[:, b % 2, LO, :, :], q["x_hi"], q["x_lo"], b)

            def split_c(b):
                pool.wait_ge(cT_in[b], 16)
                if b >= 2:
                    pool.wait_ge(q["s_ready"], b - 1)
                split(cT_sb[:, b, :, :], cs[:, b % 2, HI, :, :], cs[:, b % 2, LO, :, :], q["c_hi"], q["c_lo"], b)

            def rstd1(b):
                pool.wait_ge(q["mom1_ok"], QT * (b + 1))
                if b >= 1:
                    pool.wait_ge(q["rs1_ok"], b)
                g.tensor_scalar(var1[:, :], mom1[:, b, :, 1], float(D), EPS * D, ALU.mult, ALU.add).then_inc(q["var1_ok"], 1)
                pool.wait_ge(q["var1_ok"], b + 1)
                g.tensor_tensor(rs1[:, b, :], var1[:, :], half_neg[:, :], ALU.pow).then_inc(q["rs1_ok"], 1)

            def rstd2(b):
                pool.wait_ge(q["mom2_ok"], QT * (b + 1))
                if b >= 1:
                    pool.wait_ge(q["rs2_ok"], b)
                g.tensor_scalar(var2[:, :], mom2[:, b, :, 1], 1.0, EPS, ALU.mult, ALU.add).then_inc(q["var2_ok"], 1)
                pool.wait_ge(q["var2_ok"], b + 1)
                g.tensor_tensor(rs2[:, b, :], var2[:, :], half_neg[:, :], ALU.pow).then_inc(q["rs2_ok"], 1)

            def select_down(b):
                pool.wait_ge(q["pick_ok"], b + 1)
                e = pool.value_load(pick[0:1, b, 0:1], min_val=0, max_val=E - 1)
                if b == 0:
                    pool.wait_ge(q["dw_lo"], 1)
                    pool.wait_ge(q["bd_ok"], 16)
                    pool.wait_ge(q["dpad_ok"], 1)
                else:
                    pool.wait_ge(q["h_ready"], b)
                    pool.wait_ge(q["relu_ok"], b)
                g.tensor_copy(dsel[:, :, :, 0:R], raw(dws[:, bass.ds(e, 1), :, :, :])).then_inc(q["dsel_ok"], 1)
                g.tensor_copy(bsel[:, :], bd_aug[:, bass.ds(e, 1)]).then_inc(q["bsel_ok"], 1)
                return e

            def select_up(b, e):
                if b == 0:
                    pool.wait_ge(q["u_lo"], E // 2)
                else:
                    pool.wait_ge(q["y_ready"], b)
                g.tensor_copy(usel[:, :, :], raw(us[:, bass.ds(e, 1), :, :])).then_inc(q["usel_ok"], 1)

            def split_h(b):
                pool.wait_ge(q["relu_ok"], b + 1)
                if b >= 1:
                    pool.wait_ge(q["y_ready"], b)
                split(h_f[:, :], hs[:, HI, :], hs[:, LO, :], q["h_hi"], q["h_lo"], b)

            g.memset(half_neg[:, :], -0.5).then_inc(q["pow_ok"], 1)
            pool.wait_ge(q["pow_ok"], 1)
            g.memset(up_sb[:, :, :, R + 1:P], 0.0).then_inc(q["upad_ok"], 1)
            split_x(0)
            split_c(0)
            g.memset(row_bias[:, :, :], 0.0).then_inc(q["bias0"], 1)
            g.memset(ident_h[:, :], 0.0).then_inc(q["idh0"], 1)
            g.memset(mask_h[:, :], 0.0).then_inc(q["mask0"], 1)
            g.memset(ident[:, :], 0.0).then_inc(q["id0"], 1)
            pool.wait_ge(q["idh0"], 1)
            g.affine_select(out=ident_h[:, :], in_=ident_h[:, :], compare_op=ALU.not_equal, fill=1.0, base=0,
                            pattern=[[-1, P]], channel_multiplier=1).then_inc(q["idh_ok"], 1)
            pool.wait_ge(q["mask0"], 1)
            g.affine_select(out=mask_h[:, :], in_=mask_h[:, :], compare_op=ALU.is_ge, fill=MASKED, base=0,
                            pattern=[[-1, P]], channel_multiplier=1).then_inc(q["mask_ok"], 1)
            pool.wait_ge(q["id0"], 1)
            g.affine_select(out=ident[:, :], in_=ident[:, :], compare_op=ALU.not_equal, fill=1.0, base=0,
                            pattern=[[-1, P]], channel_multiplier=1).then_inc(q["id_ok"], 1)
            rstd1(0)
            split_x(1)
            split_c(1)
            g.memset(bd_aug[:, :], 0.0).then_inc(q["bd0"], 1)
            pool.wait_ge(q["bd0"], 1)
            g.memset(bd_aug[R:R + 1, :], 1.0).then_inc(q["bd0"], 1)
            pool.wait_ge(q["bd0"], 2)
            g.memset(raw(dsel[:, :, :, :]), 0.0).then_inc(q["dpad_ok"], 1)
            pool.wait_ge(q["dpad_ok"], 1)
            pool.wait_ge(bias_in, 32)
            g.tensor_tensor(row_bias[R:R + 1, :, :], row_bias[R:R + 1, :, :],
                            base_row[R:R + 1, :].rearrange("p (a d) -> p a d", a=1).broadcast_to((1, E, D)),
                            ALU.add).then_inc(q["bias_ok"], 1)
            pool.wait_ge(q["bias_ok"], 1)
            rstd1(1)
            pool.wait_ge(wb_in, 16)
            split(wb_sb[:, :, :], wbs[HI][:, :, :], wbs[LO][:, :, :], q["wb_hi"], q["wb_lo"], 0)

            for i in range(0, B + 2):
                if i >= 2:
                    e = select_down(i - 2)
                if 1 <= i <= B:
                    rstd2(i - 1)
                if i >= 2:
                    select_up(i - 2, e)
                if i + 2 < B:
                    split_x(i + 2)
                if i >= 2:
                    split_h(i - 2)
                if i + 2 < B:
                    split_c(i + 2)
                    rstd1(i + 2)

        @block.scalar
        def _(act):
            a = nc.scalar

            def copy_hi(hi, src, done):
                a.activation(hi, src, ACT.Copy).then_inc(done, 1)

            def t_hi(b):
                act.wait_ge(q["t_ready"], b + 1)
                copy_hi(ts[:, HI, :, :], t_ps, q["t_hi"])

            def v_hi(b):
                act.wait_ge(q["v_ready"], b + 1)
                if b >= 2:
                    act.wait_ge(q["o_ready"], b - 1)
                copy_hi(vs[:, b % 2, HI, :, :], v_ps, q["v_hi"])

            def exps(b):
                act.wait_ge(q["nmax_ok"], b + 1)
                if b >= 1:
                    act.wait_ge(q["pt_ready"], b)
                a.activation(prob[:, 0:P], ps_s[:, 0:P], ACT.Exp, bias=nmax[:, b, 0:1], scale=rs1[:, b, 0:1],
                             accum_out=rsum[:, b, 0:1]).then_inc(q["exp_ok"], 1)
                a.activation(prob[:, P:SC], ps_s[:, P:SC], ACT.Exp, bias=nmax[:, b, 1:2], scale=rs1[:, b, 1:2],
                             accum_out=rsum[:, b, 1:2]).then_inc(q["exp_ok"], 1)

            def pt_hi(b):
                act.wait_ge(q["pt_ready"], b + 1)
                if b >= 1:
                    act.wait_ge(q["o_ready"], b)
                copy_hi(pts[:, HI, :], ps_s[:, 0:SC], q["pt_hi"])

            def relu(b):
                act.wait_ge(q["h_ready"], b + 1)
                act.wait_ge(q["bsel_ok"], b + 1)
                if b >= 1:
                    act.wait_ge(q["h_lo"], b)
                a.activation(h_f[:, :], h_ps, ACT.Relu, bias=bsel[:, 0:1]).then_inc(q["relu_ok"], 1)

            def z_hi(b):
                act.wait_ge(q["z_ready"], b + 1)
                if b >= 2:
                    act.wait_ge(q["h_ready"], b - 1)
                for k in range(KD):
                    a.activation(zs[:, b % 2, HI, k, :], z_ps[:, k, :], ACT.Copy,
                                 accum_out=pooled[:, b, k:k + 1]).then_inc(q["z_hi"], 1)
                for k in range(KD):
                    if b + k >= 1:
                        act.wait_ge(q["z_sq"], KD * b + k)
                    a.activation(sq[:, :], z_ps[:, k, :], ACT.Square,
                                 accum_out=pooled[:, b, KD + k:KD + k + 1]).then_inc(q["z_sq"], 1)

            act.wait_ge(q["mc_ready"], 1)
            copy_hi(mc[HI][:, :, :], t_ps, q["mc_hi"])
            act.wait_ge(wv_in, 16)
            copy_hi(wvs[HI][:, :, :], wv_sb[:, :, :], q["wv_hi"])
            for i in range(-1, B + 2):
                if 0 <= i < B:
                    exps(i)
                if i + 1 < B:
                    t_hi(i + 1)
                if 0 <= i < B:
                    pt_hi(i)
                if i >= 2:
                    relu(i - 2)
                if 1 <= i <= B:
                    z_hi(i - 1)
                if i + 1 < B:
                    v_hi(i + 1)
                if i in (0, 1):
                    if i == 1:
                        act.wait_ge(down_in, 16 * E)
                        copy_hi(dws[:, :, HI, :, :], dw_sb[:, :, :, :], q["dw_hi"])
                    for j in (2 * i, 2 * i + 1):
                        act.wait_ge(q["u_sum"], j + 1)
                        copy_hi(us[:, 2 * j:2 * j + 2, HI, :], u_f[:, :, :], q["u_hi"])

        @block.vector
        def _(dve):
            v = nc.vector

            def sub_lo(lo, src, hi, done):
                v.tensor_tensor(lo, src, raw(hi), ALU.subtract).then_inc(done, 1)

            def moments(src, stats, mom, b, st_ok, mom_ok):
                for t in range(QT):
                    v.bn_stats(stats[:, b % 2, t, :], src[:, b, t, :]).then_inc(st_ok, 1)
                for t in range(QT):
                    dve.wait_ge(st_ok, QT * b + t + 1)
                    v.bn_aggr(mom[:, b, t, :], stats[:, b % 2, t, :]).then_inc(mom_ok, 1)

            def moments1(b):
                dve.wait_ge(x_in[b], 16)
                if b >= 2:
                    dve.wait_ge(q["mom1_ok"], QT * (b - 1))
                moments(x_sb, stats1, mom1, b, q["st1_ok"], q["mom1_ok"])

            def argmin(b):
                dve.wait_ge(q["l_ready"], b + 1)
                v.tensor_tensor(nloss[:, b, :], l_ps, loss_c[:, :], ALU.add).then_inc(q["nloss_ok"], 1)
                dve.wait_ge(q["nloss_ok"], b + 1)
                v.max(best[:, b, :], nloss[:, b, :]).then_inc(q["best_ok"], 1)
                dve.wait_ge(q["best_ok"], b + 1)
                v.max_index(pick[:, b, :], best[:, b, :], nloss[:, b, :]).then_inc(q["pick_ok"], 1)

            def row_max(b):
                dve.wait_ge(q["s_ready"], b + 1)
                v.reduce_max(rmax[:, b, 0:1], ps_s[:, 0:P], AX.X).then_inc(q["max_ok"], 1)
                v.reduce_max(rmax[:, b, 1:2], ps_s[:, P:SC], AX.X).then_inc(q["max_ok"], 1)
                dve.wait_ge(q["max_ok"], QT * (b + 1))
                dve.wait_ge(q["rs1_ok"], b + 1)
                v.scalar_tensor_tensor(out=nmax[:, b, :], in0=rmax[:, b, :], scalar=-1.0, in1=rs1[:, b, :],
                                       op0=ALU.mult, op1=ALU.mult).then_inc(q["nmax_ok"], 1)

            def normalize(b):
                dve.wait_ge(q["rs2_ok"], b + 1)
                if b >= 1:
                    dve.wait_ge(q["z_ready"], b)
                for t in range(QT):
                    v.tensor_scalar(z[:, t, :], x2[:, b, t, :], mom2[:, b, t, 0:1], rs2[:, b, t:t + 1],
                                    ALU.subtract, ALU.mult).then_inc(q["z_ok"], 1)

            def t_lo(b):
                dve.wait_ge(q["t_hi"], b + 1)
                sub_lo(ts[:, LO, :, :], t_ps, ts[:, HI, :, :], q["t_lo"])

            def v_lo(b):
                dve.wait_ge(q["v_hi"], b + 1)
                sub_lo(vs[:, b % 2, LO, :, :], v_ps, vs[:, b % 2, HI, :, :], q["v_lo"])

            def pt_lo(b):
                dve.wait_ge(q["pt_hi"], b + 1)
                sub_lo(pts[:, LO, :], ps_s[:, 0:SC], pts[:, HI, :], q["pt_lo"])

            def z_lo(b):
                dve.wait_ge(q["z_sq"], KD * (b + 1))
                sub_lo(zs[:, b % 2, LO, :, :], z_ps, zs[:, b % 2, HI, :, :], q["z_lo"])

            def residual(b):
                dve.wait_ge(q["exp_ok"], QT * (b + 1))
                v.reciprocal(rinv[:, b, :], rsum[:, b, :]).then_inc(q["rinv_ok"], 1)
                dve.wait_ge(q["rinv_ok"], b + 1)
                dve.wait_ge(q["o_ready"], b + 1)
                for t in range(QT):
                    v.scalar_tensor_tensor(out=x2[:, b, t, :], in0=o_ps[:, t, :], scalar=rinv[:, b, t:t + 1],
                                           in1=x_sb[:, b, t, :], op0=ALU.mult, op1=ALU.add).then_inc(q["x2_ok"], 1)

            def moments2(b):
                dve.wait_ge(q["x2_ok"], QT * (b + 1))
                if b >= 2:
                    dve.wait_ge(q["mom2_ok"], QT * (b - 1))
                moments(x2, stats2, mom2, b, q["st2_ok"], q["mom2_ok"])

            def finish(b):
                dve.wait_ge(q["y_ready"], b + 1)
                dve.wait_ge(q["z_ok"], QT * (b + 1))
                v.tensor_tensor(x2[:, b, :, :], y_ps[b % 2], x2[:, b, :, :], ALU.add).then_inc(q["fin_ok"], 1)

            def fold_sum(j):
                dve.wait_ge(q["u_ready"], j + 1)
                dve.wait_ge(q["bias_ok"], 1)
                if j >= 1:
                    dve.wait_ge(q["u_lo"], j)
                bank = (ps_h if j % 2 == 0 else ps_y[1])[:, :].rearrange("p (e d) -> p e d", e=2)
                v.tensor_tensor(u_f[:, :, :], bank, row_bias[:, 2 * j:2 * j + 2, :], ALU.add).then_inc(q["u_sum"], 1)
                dve.wait_ge(q["u_hi"], j + 1)
                sub_lo(us[:, 2 * j:2 * j + 2, LO, :], u_f[:, :, :], us[:, 2 * j:2 * j + 2, HI, :], q["u_lo"])

            v.memset(ones_col[:, :], 1.0).then_inc(q["ones_ok"], 1)
            dve.wait_ge(wq_in, 16)
            v.reduce_sum(wq_sum[:, :], wqT_sb[:, :, :], AX.X).then_inc(q["wq_summed"], 1)
            dve.wait_ge(q["wq_summed"], 1)
            v.tensor_scalar(wq_sum[:, :], wq_sum[:, :], 1.0 / D, None, ALU.mult).then_inc(q["wq_meaned"], 1)
            dve.wait_ge(q["wq_meaned"], 1)
            for k in range(KD):
                v.tensor_scalar(wqc[:, k, :], wqT_sb[:, k, :], wq_sum[:, k:k + 1], None,
                                ALU.subtract).then_inc(q["wqc_ok"], 1)
            dve.wait_ge(q["mc_hi"], 1)
            sub_lo(mc[LO][:, :, :], t_ps, mc[HI][:, :, :], q["mc_lo"])
            moments1(0)
            dve.wait_ge(q["wv_hi"], 1)
            sub_lo(wvs[LO][:, :, :], wv_sb[:, :, :], wvs[HI][:, :, :], q["wv_lo"])
            for i in range(-1, B + 2):
                if i >= 2:
                    argmin(i - 2)
                if 0 <= i < B:
                    row_max(i)
                if 1 <= i <= B:
                    normalize(i - 1)
                if i + 1 < B:
                    t_lo(i + 1)
                if 0 <= i < B:
                    pt_lo(i)
                if 1 <= i <= B:
                    z_lo(i - 1)
                if i + 1 < B:
                    v_lo(i + 1)
                if i + 2 < B:
                    moments1(i + 2)
                if 0 <= i < B:
                    residual(i)
                if i >= 2:
                    finish(i - 2)
                if 0 <= i < B:
                    moments2(i)
                if i == 0:
                    dve.wait_ge(disc_in, 32)
                    v.tensor_tensor(sg2[:, :, :], sg_sb[:, :, :], sg_sb[:, :, :], ALU.mult).then_inc(q["sg2_ok"], 1)
                    dve.wait_ge(q["sg2_ok"], 1)
                    v.reciprocal(inv_var[:, :, :], sg2[:, :, :]).then_inc(q["iv_ok"], 1)
                    dve.wait_ge(q["iv_ok"], 1)
                    v.tensor_tensor(mu_iv[:, :, :], mu_sb[:, :, :], inv_var[:, :, :], ALU.mult).then_inc(q["muiv_ok"], 1)
                    dve.wait_ge(q["muiv_ok"], 1)
                    v.tensor_scalar(tab_m2[:, :, :], inv_var[:, :, :], -1.0 / S, None, ALU.mult).then_inc(q["tab_ok"], 1)
                    v.tensor_scalar(tab_m1[:, :, :], mu_iv[:, :, :], 2.0 / S, None, ALU.mult).then_inc(q["tab_ok"], 1)
                    v.scalar_tensor_tensor(out=tab_c[:, :, :], in0=mu_iv[:, :, :], scalar=-1.0, in1=mu_sb[:, :, :],
                                           op0=ALU.mult, op1=ALU.mult).then_inc(q["tab_ok"], 1)
                    fold_sum(0)
                    fold_sum(1)
                if i == 1:
                    dve.wait_ge(q["dw_hi"], 1)
                    sub_lo(dws[:, :, LO, :, :], dw_sb[:, :, :, :], dws[:, :, HI, :, :], q["dw_lo"])
                    fold_sum(2)
                    fold_sum(3)
                    dve.wait_ge(q["lossc_ready"], 1)
                    v.tensor_copy(loss_c[:, :], l_ps).then_inc(q["lossc_ok"], 1)
                    dve.wait_ge(q["lossc_ok"], 1)

        @block.tensor
        def _(pe):
            t = nc.tensor

            def mm(dst, lhsT, rhs, start, stop):
                return t.matmul(dst, lhsT, rhs, start=start, stop=stop, skip_group_check=True)

            def mm_split(dst, lhs, rhs, start, stop):
                mm(dst, lhs[LO], rhs[HI], start, False)
                mm(dst, lhs[HI], rhs[LO], False, False)
                return mm(dst, lhs[HI], rhs[HI], False, stop)

            def halves(tile, *at):
                return [tile[(slice(None),) + at[:-1] + (h,) + tuple(at[-1])] for h in (HI, LO)]

            def project_t(b):
                pe.wait_ge(q["x_lo"], b + 1)
                if b == 0:
                    pe.wait_ge(q["mc_lo"], 1)
                else:
                    pe.wait_ge(q["t_lo"], b)
                for m in range(KD):
                    for k in range(KD):
                        last = mm_split(t_ps[:, m, :], [mc[h][:, k, m * P:(m + 1) * P] for h in (HI, LO)],
                                        [xs[:, b % 2, h, k, :] for h in (HI, LO)], k == 0, k == KD - 1)
                last.then_inc(q["t_ready"], 1)

            def project_v(b):
                pe.wait_ge(q["c_lo"], b + 1)
                if b == 0:
                    pe.wait_ge(q["wv_lo"], 1)
                else:
                    pe.wait_ge(q["v_lo"], b)
                for m in range(QT):
                    for k in range(KD):
                        last = mm_split(v_ps[:, m, :], [cs[:, b % 2, h, k, m * P:(m + 1) * P] for h in (HI, LO)],
                                        [wvs[h][:, k, :] for h in (HI, LO)], k == 0, k == KD - 1)
                last.then_inc(q["v_ready"], 1)

            def scores(b):
                pe.wait_ge(q["t_lo"], b + 1)
                pe.wait_ge(q["c_lo"], b + 1)
                if b == 0:
                    pe.wait_ge(q["idh_ok"], 1)
                    pe.wait_ge(q["mask_ok"], 1)
                else:
                    pe.wait_ge(q["pt_lo"], b)
                for m in range(QT):
                    lo = 0 if m == 0 else P
                    keys = (m + 1) * P
                    dst = ps_s[:, lo:lo + keys]
                    for k in range(KD):
                        mm_split(dst, [ts[:, h, k, m * P:(m + 1) * P] for h in (HI, LO)],
                                 [cs[:, b % 2, h, k, 0:keys] for h in (HI, LO)], k == 0, False)
                    last = mm(ps_s[:, lo + keys - P:lo + keys], ident_h[:, :], mask_h[:, :], False, True)
                last.then_inc(q["s_ready"], 1)

            def transpose_p(b):
                pe.wait_ge(q["exp_ok"], QT * (b + 1))
                if b == 0:
                    pe.wait_ge(q["id_ok"], 1)
                for j in range(SC // P):
                    last = t.transpose(ps_s[:, j * P:(j + 1) * P], prob[:, j * P:(j + 1) * P], ident[:, :])
                last.then_inc(q["pt_ready"], 1)

            def attend(b):
                pe.wait_ge(q["pt_lo"], b + 1)
                pe.wait_ge(q["v_lo"], b + 1)
                if b >= 1:
                    pe.wait_ge(q["x2_ok"], QT * b)
                for m, j, k, first, stop in ((0, 0, 0, True, True), (1, 1, 0, True, False), (1, 2, 1, False, True)):
                    last = mm_split(o_ps[:, m, :], [pts[:, h, j * P:(j + 1) * P] for h in (HI, LO)],
                                    [vs[:, b % 2, h, k, :] for h in (HI, LO)], first, stop)
                last.then_inc(q["o_ready"], 1)

            def transpose_z(b):
                pe.wait_ge(q["z_ok"], QT * (b + 1))
                if b >= 1:
                    pe.wait_ge(q["z_lo"], b)
                for k in range(KD):
                    for m in range(QT):
                        last = t.transpose(z_ps[:, k, m * P:(m + 1) * P], z[:, m, k * P:(k + 1) * P], ident[:, :])
                last.then_inc(q["z_ready"], 1)

            def base(b):
                pe.wait_ge(q["z_lo"], b + 1)
                if b == 0:
                    pe.wait_ge(q["wb_lo"], 1)
                if b == 1:
                    pe.wait_ge(q["u_sum"], E // 2)
                if b >= 2:
                    pe.wait_ge(q["fin_ok"], b - 1)
                for m in range(QT):
                    for k in range(KD):
                        mm_split(y_ps[b % 2][:, m, :],
                                 [zs[:, b % 2, h, k, m * P:(m + 1) * P] for h in (HI, LO)],
                                 [wbs[h][:, k, :] for h in (HI, LO)], m == 0 and k == 0, False)

            def losses(b):
                pe.wait_ge(q["z_sq"], KD * (b + 1))
                if b == 0:
                    pe.wait_ge(q["lossc_ok"], 1)
                else:
                    pe.wait_ge(q["relu_ok"], b)
                    pe.wait_ge(q["nloss_ok"], b)
                tabs = [tab_m1, tab_m2]
                for j in range(2 * KD):
                    last = mm(l_ps, pooled[:, b, j:j + 1], tabs[j // KD][:, j % KD, :], j == 0, j == 2 * KD - 1)
                last.then_inc(q["l_ready"], 1)

            def down(b):
                pe.wait_ge(q["dsel_ok"], b + 1)
                pe.wait_ge(q["nloss_ok"], b + 1)
                for k in range(KD):
                    last = mm_split(h_ps, [dsel[:, h, k, :] for h in (HI, LO)],
                                    [zs[:, b % 2, h, k, :] for h in (HI, LO)], k == 0, k == KD - 1)
                last.then_inc(q["h_ready"], 1)

            def expert(b):
                pe.wait_ge(q["h_lo"], b + 1)
                pe.wait_ge(q["usel_ok"], b + 1)
                for m in range(QT):
                    last = mm_split(y_ps[b % 2][:, m, :], [hs[:, h, m * P:(m + 1) * P] for h in (HI, LO)],
                                    [usel[:, h, :] for h in (HI, LO)], False, m == QT - 1)
                last.then_inc(q["y_ready"], 1)

            def fold(j):
                pe.wait_ge(up_in[j // 2], 64)
                pe.wait_ge(conv_in[j], 32)
                if j >= 2:
                    pe.wait_ge(q["u_sum"], j - 1)
                bank = ps_h if j % 2 == 0 else ps_y[1]
                for s, e in enumerate((2 * j, 2 * j + 1)):
                    for k in range(KD):
                        last = mm(bank[:, s * D:(s + 1) * D], up_sb[:, e, k, :], cw_sb[:, e, k, :],
                                  k == 0, k == KD - 1)
                last.then_inc(q["u_ready"], 1)

            pe.wait_ge(wk_in, 16)
            pe.wait_ge(q["wqc_ok"], KD)
            for m in range(KD):
                for k in range(KD):
                    last = mm(t_ps[:, m, :], wqc[:, k, m * P:(m + 1) * P], wkT_sb[:, k, :], k == 0, k == KD - 1)
            last.then_inc(q["mc_ready"], 1)
            for i in range(-1, B + 2):
                if 0 <= i < B:
                    scores(i)
                if i + 1 < B:
                    project_t(i + 1)
                if 0 <= i < B:
                    transpose_p(i)
                if i >= 2:
                    down(i - 2)
                if 1 <= i <= B:
                    transpose_z(i - 1)
                if i + 1 < B:
                    project_v(i + 1)
                if 0 <= i < B:
                    attend(i)
                if i >= 2:
                    expert(i - 2)
                if i == 0:
                    fold(0)
                    fold(1)
                if i == 1:
                    fold(2)
                    fold(3)
                    pe.wait_ge(q["tab_ok"], 3)
                    pe.wait_ge(q["ones_ok"], 1)
                    pe.wait_ge(q["u_sum"], 3)
                    for k in range(KD):
                        last = mm(l_ps, ones_col[:, :], tab_c[:, k, :], k == 0, k == KD - 1)
                    last.then_inc(q["lossc_ready"], 1)
                if 1 <= i <= B:
                    base(i - 1)
                    losses(i - 1)


_INS = ["x", "xT", "ctxT", "wqT", "wkT", "wv", "base_wT", "mu_T", "sigma_T",
        "down_w", "down_bT", "up_aug", "conv_wT", "conv_b", "base_b"]


def kernel(**inputs):
    import numpy as _np
    import concourse.bacc as _bacc
    from concourse import mybir as _mybir
    from concourse.bass_utils import run_bass_kernel_spmd as _run

    a = {n: _np.asarray(v) for n, v in inputs.items()}
    laid = {
        "x": a["x"],
        "xT": a["x"].transpose(0, 2, 1),
        "ctxT": a["ctx_1024"].transpose(0, 2, 1),
        "wqT": a["L0_xattn_w_q"].T,
        "wkT": a["L0_xattn_w_k"].T,
        "wv": a["L0_xattn_w_v"],
        "base_wT": a["L0_ffn_base_W"].T,
        "mu_T": a["L0_ffn_disc_mu"].T,
        "sigma_T": a["L0_ffn_disc_sigma"].T,
        "down_w": a["L0_ffn_down_W"],
        "down_bT": a["L0_ffn_down_b"].T,
        "up_aug": _np.concatenate([a["L0_ffn_up_W"].transpose(0, 2, 1), a["L0_ffn_up_b"][:, :, None]], axis=2),
        "conv_wT": a["L0_ffn_conv_W"].transpose(0, 2, 1),
        "conv_b": a["L0_ffn_conv_b"],
        "base_b": a["L0_ffn_base_b"],
    }
    nc = _bacc.Bacc("TRN2", target_bir_lowering=False, num_devices=1)
    arrays, args = {}, []
    for name in _INS:
        arr = _np.ascontiguousarray(laid[name])
        arrays[f"in_{name}"] = arr
        args.append(nc.dram_tensor(f"in_{name}", arr.shape, _mybir.dt.from_np(arr.dtype), kind="ExternalInput").ap())
    out = nc.dram_tensor("out_0", a["x"].shape, _mybir.dt.from_np(a["x"].dtype), kind="ExternalOutput").ap()
    xattn_ffn_program(nc, *args, out)
    r = _run(nc, [arrays], core_ids=[0])
    return r.results[0]["out_0"]
```

```python
import numpy as np
import concourse.bass as bass
from concourse import mybir
from contextlib import ExitStack


def xattn_ffn_program(nc, x, xT, ctxT, wqT, wkT, wv, base_wT, mu_T, sigma_T,
                      down_w, down_bT, up_aug, conv_wT, conv_b, base_b, out):
    f32 = mybir.dt.float32
    f32r = mybir.dt.float32r
    bf16 = mybir.dt.bfloat16
    u32 = mybir.dt.uint32
    ALU = mybir.AluOpType
    ACT = mybir.ActivationFunctionType
    AX = mybir.AxisListType

    P = 128
    B, S, D = x.shape
    E, R = down_w.shape[0], down_w.shape[2]
    KD = D // P
    QT = S // P
    SC = P * (1 + 2)
    EPS = 1e-5
    MASKED = -1e30
    HI, LO = 0, 1
    WARM = 10

    ctx = ExitStack()
    with ctx:
        def sb(name, shape, dt=f32):
            return ctx.enter_context(nc.sbuf_tensor(name, shape, dt))

        def pb(name, shape=(P, 512)):
            return ctx.enter_context(nc.psum_tensor(name, list(shape), f32))

        def sem(name):
            return ctx.enter_context(nc.semaphore(name))

        x_sb = sb("x_sb", [P, B, QT, D])
        xT_sb = sb("xT_sb", [P, B, KD, S])
        cT_sb = sb("cT_sb", [P, B, KD, S])
        wqT_sb = sb("wqT_sb", [P, KD, D])
        wkT_sb = sb("wkT_sb", [P, KD, D])
        wv_sb = sb("wv_sb", [P, KD, D])
        wb_sb = sb("wb_sb", [P, KD, D])
        mu_sb = sb("mu_sb", [P, KD, E])
        sg_sb = sb("sg_sb", [P, KD, E])
        dw_sb = sb("dw_sb", [P, E, KD, R])
        up_sb = sb("up_sb", [P, E, KD, P])
        cw_sb = sb("cw_sb", [P, E, KD, D])
        row_bias = sb("row_bias", [P, E, D])
        base_row = sb("base_row", [P, D])
        bd_aug = sb("bd_aug", [P, E])
        ident = sb("ident", [P, P])
        ident_h = sb("ident_h", [P, P], bf16)
        mask_h = sb("mask_h", [P, P], bf16)
        half_neg = sb("half_neg", [P, 2 * QT])
        ones_col = sb("ones_col", [P, 1])
        warm = sb("warm", [P, 4 * P], bf16)
        wq_sum = sb("wq_sum", [P, KD])
        wqc = sb("wqc", [P, KD, D])
        mc = [sb(f"mc{h}", [P, KD, D], f32r) for h in (HI, LO)]
        wvs = [sb(f"wvs{h}", [P, KD, D], f32r) for h in (HI, LO)]
        wbs = [sb(f"wbs{h}", [P, KD, D], f32r) for h in (HI, LO)]
        dws = sb("dws", [P, E, 2, KD, R], f32r)
        u_f = sb("u_f", [P, 2, 2, D])
        us = sb("us", [P, E, 2, D], f32r)
        sg2 = sb("sg2", [P, KD, E])
        inv_var = sb("inv_var", [P, KD, E])
        mu_iv = sb("mu_iv", [P, KD, E])
        tab_m1 = sb("tab_m1", [P, KD, E])
        tab_m2 = sb("tab_m2", [P, KD, E])
        tab_c = sb("tab_c", [P, KD, E])
        loss_c = sb("loss_c", [1, E])
        xs = sb("xs", [P, 2, 2, KD, S], f32r)
        cs = sb("cs", [P, 2, 2, KD, S], f32r)
        ts = sb("ts", [P, 2, KD, S], f32r)
        vs = sb("vs", [P, 2, 2, QT, D], f32r)
        prob = sb("prob", [P, SC])
        pts = sb("pts", [P, 2, SC], f32r)
        stats1 = sb("stats1", [P, 2, QT, 6])
        mom1 = sb("mom1", [P, B, QT, 2])
        var1 = sb("var1", [P, 2 * QT])
        rs1 = sb("rs1", [P, B, QT])
        rmax = sb("rmax", [P, B, QT])
        nmax = sb("nmax", [P, B, QT])
        rsum = sb("rsum", [P, B, QT])
        rinv = sb("rinv", [P, B, QT])
        x2 = sb("x2", [P, B, QT, D])
        stats2 = sb("stats2", [P, 2, QT, 6])
        mom2 = sb("mom2", [P, B, QT, 2])
        var2 = sb("var2", [P, QT])
        negm = sb("negm", [P, QT])
        nm2 = sb("nm2", [P, B, QT])
        rs2 = sb("rs2", [P, B, QT])
        z = sb("z", [P, QT, D])
        zs = sb("zs", [P, 2, 2, KD, S], f32r)
        sq = sb("sq", [P, S])
        pooled = sb("pooled", [P, B, 2 * KD])
        nloss = sb("nloss", [1, B, E])
        best = sb("best", [1, B, 8])
        pick = sb("pick", [1, B, 8], u32)
        dsel = sb("dsel", [P, 2, KD, P], f32r)
        h_f = sb("h_f", [P, S])
        hs = sb("hs", [P, 2, S], f32r)

        ps_t, ps_v, ps_s, ps_o, ps_z, ps_h = [pb(n) for n in ("ps_t", "ps_v", "ps_s", "ps_o", "ps_z", "ps_h")]
        ps_y = [pb("ps_y0"), pb("ps_y1")]
        t_ps = ps_t[:, :].rearrange("p (k s) -> p k s", k=KD)
        v_ps = ps_v[:, :].rearrange("p (k s) -> p k s", k=QT)
        o_ps = ps_o[:, :].rearrange("p (t d) -> p t d", t=QT)
        z_ps = ps_z[:, :].rearrange("p (k s) -> p k s", k=KD)
        h_ps = ps_h[:, 0:S]
        l_ps = ps_h[0:1, S:S + E]
        y_ps = [t[:, :].rearrange("p (t d) -> p t d", t=QT) for t in ps_y]

        fold_bank = [ps_h, ps_y[1], ps_y[0]]
        FB = len(fold_bank)

        wq_in, wk_in, wv_in, wb_in = sem("wq_in"), sem("wk_in"), sem("wv_in"), sem("wb_in")
        disc_in, down_in, bias_in = sem("disc_in"), sem("down_in"), sem("bias_in")
        up_in = [sem(f"up_in{j}") for j in range(2)]
        conv_in = [sem(f"conv_in{j}") for j in range(4)]
        xT_in = [sem(f"xT_in{b}") for b in range(B)]
        cT_in = [sem(f"cT_in{b}") for b in range(B)]
        x_in = [sem(f"x_in{b}") for b in range(B)]
        stored = sem("stored")
        names = ("warm_ok id0 id_ok idh0 idh_ok mask0 mask_ok pow_ok ones_ok dpad_ok upad_ok bd0 bd_ok bias0 bias_ok "
                 "wq_summed wq_meaned wqc_ok mc_ready mc_hi mc_lo wv_hi wv_lo wb_hi wb_lo dw_hi dw_lo "
                 "sg2_ok iv_ok muiv_ok tab_ok lossc_ready lossc_ok u_ready u_sum u_hi u_lo "
                 "x_hi x_lo c_hi c_lo t_ready t_hi t_lo v_ready v_hi v_lo st1_ok mom1_ok var1_ok rs1_ok "
                 "s_ready max_ok nmax_ok exp_ok pt_ready pt_hi pt_lo o_ready rinv_ok x2_ok st2_ok mom2_ok "
                 "var2_ok negm_ok rs2_ok nm2_ok z_ok z_ready z_hi z_sq z_lo l_ready nloss_ok best_ok pick_ok dsel_ok "
                 "h_ready relu_ok h_hi h_lo base_ready y_ready fin_ok").split()
        q = {n: sem(n) for n in names}

        def raw(ap):
            return ap.bitcast(f32)

        block = ctx.enter_context(nc.Block())

        @block.sync
        def _(sp):
            def weights(dst, src, done):
                sp.dma_start(dst[:, :, :], src.rearrange("(k p) n -> p k n", p=P)).then_inc(done, 16)

            def transposed(dst, src, b, done):
                sp.dma_start(dst[:, b, :, :], src[b].rearrange("(k p) s -> p k s", p=P)).then_inc(done[b], 16)

            def natural(b):
                sp.dma_start(x_sb[:, b, :, :], x[b].rearrange("(t p) d -> p t d", p=P)).then_inc(x_in[b], 16)

            def batch(b):
                transposed(xT_sb, xT, b, xT_in)
                transposed(cT_sb, ctxT, b, cT_in)
                natural(b)

            def fold_weights(j):
                es = slice(4 * j, 4 * j + 4)
                sp.dma_start(up_sb[:, es, :, 0:R + 1],
                             up_aug[es].rearrange("e (k p) r -> p e k r", p=P)).then_inc(up_in[j], 16)
                for i in (2 * j, 2 * j + 1):
                    sp.dma_start(cw_sb[:, 2 * i:2 * i + 2, :, :],
                                 conv_wT[2 * i:2 * i + 2].rearrange("e (k p) o -> p e k o", p=P)).then_inc(conv_in[i], 16)

            weights(wqT_sb, wqT, wq_in)
            weights(wkT_sb, wkT, wk_in)
            transposed(cT_sb, ctxT, 0, cT_in)
            weights(wv_sb, wv, wv_in)
            transposed(xT_sb, xT, 0, xT_in)
            transposed(cT_sb, ctxT, 1, cT_in)
            natural(0)
            transposed(xT_sb, xT, 1, xT_in)
            natural(1)
            sp.wait_ge(q["upad_ok"], 1)
            fold_weights(0)
            weights(wb_sb, base_wT, wb_in)
            batch(2)
            fold_weights(1)
            sp.dma_start(dw_sb[:, :, :, :], down_w.rearrange("e (k p) r -> p e k r", p=P)).then_inc(down_in, 16)
            sp.wait_ge(q["bd0"], 2)
            sp.dma_start(bd_aug[0:R, :], down_bT).then_inc(q["bd_ok"], 16)
            for b in range(3, B):
                batch(b)
            for b in range(B):
                sp.wait_ge(q["fin_ok"], b + 1)
                sp.dma_start(out[b].rearrange("(t p) d -> p t d", p=P), x2[:, b, :, :]).then_inc(stored, 16)
            sp.wait_ge(stored, 16 * B)

        @block.gpsimd
        def _(pool):
            g = nc.gpsimd

            def sub_lo(lo, src, hi, done):
                g.tensor_tensor(lo, src, raw(hi), ALU.subtract).then_inc(done, 1)

            def x_lo(b):
                pool.wait_ge(q["x_hi"], b + 1)
                sub_lo(xs[:, b % 2, LO, :, :], xT_sb[:, b, :, :], xs[:, b % 2, HI, :, :], q["x_lo"])

            def c_lo(b):
                pool.wait_ge(q["c_hi"], b + 1)
                sub_lo(cs[:, b % 2, LO, :, :], cT_sb[:, b, :, :], cs[:, b % 2, HI, :, :], q["c_lo"])

            def rstd1(b):
                pool.wait_ge(q["mom1_ok"], QT * (b + 2))
                if b >= 2:
                    pool.wait_ge(q["rs1_ok"], b // 2)
                g.tensor_scalar(var1[:, :], mom1[:, b:b + 2, :, 1], float(D), EPS * D, ALU.mult, ALU.add).then_inc(q["var1_ok"], 1)
                pool.wait_ge(q["var1_ok"], b // 2 + 1)
                g.tensor_tensor(rs1[:, b:b + 2, :], var1[:, :], half_neg[:, :], ALU.pow).then_inc(q["rs1_ok"], 1)

            def rstd2(b):
                pool.wait_ge(q["mom2_ok"], QT * (b + 1))
                if b >= 1:
                    pool.wait_ge(q["rs2_ok"], b)
                    pool.wait_ge(q["nm2_ok"], b)
                g.tensor_scalar(var2[:, :], mom2[:, b, :, 1], 1.0, EPS, ALU.mult, ALU.add).then_inc(q["var2_ok"], 1)
                g.tensor_scalar(negm[:, :], mom2[:, b, :, 0], -1.0, 0.0, ALU.mult, ALU.add).then_inc(q["negm_ok"], 1)
                pool.wait_ge(q["var2_ok"], b + 1)
                g.tensor_tensor(rs2[:, b, :], var2[:, :], half_neg[:, 0:QT], ALU.pow).then_inc(q["rs2_ok"], 1)
                pool.wait_ge(q["rs2_ok"], b + 1)
                pool.wait_ge(q["negm_ok"], b + 1)
                g.tensor_tensor(nm2[:, b, :], negm[:, :], rs2[:, b, :], ALU.mult).then_inc(q["nm2_ok"], 1)

            def normalize(b):
                pool.wait_ge(q["nm2_ok"], b + 1)
                pool.wait_ge(q["x2_ok"], QT * (b + 1))
                if b >= 1:
                    pool.wait_ge(q["z_ready"], b)
                for t in range(1 if b == B - 1 else QT):
                    g.tensor_scalar(z[:, t, :], x2[:, b, t, :], rs2[:, b, t:t + 1], nm2[:, b, t:t + 1],
                                    ALU.mult, ALU.add).then_inc(q["z_ok"], 1)

            def h_lo(b):
                pool.wait_ge(q["relu_ok"], b + 1)
                pool.wait_ge(q["h_hi"], b + 1)
                sub_lo(hs[:, LO, :], h_f[:, :], hs[:, HI, :], q["h_lo"])

            g.memset(row_bias[:, :, :], 0.0).then_inc(q["bias0"], 1)
            g.memset(half_neg[:, :], -0.5).then_inc(q["pow_ok"], 1)
            g.memset(up_sb[:, :, :, R + 1:P], 0.0).then_inc(q["upad_ok"], 1)
            g.memset(ident_h[:, :], 0.0).then_inc(q["idh0"], 1)
            g.memset(mask_h[:, :], 0.0).then_inc(q["mask0"], 1)
            g.memset(ident[:, :], 0.0).then_inc(q["id0"], 1)
            pool.wait_ge(q["idh0"], 1)
            g.affine_select(out=ident_h[:, :], in_=ident_h[:, :], compare_op=ALU.not_equal, fill=1.0, base=0,
                            pattern=[[-1, P]], channel_multiplier=1).then_inc(q["idh_ok"], 1)
            pool.wait_ge(q["mask0"], 1)
            g.affine_select(out=mask_h[:, :], in_=mask_h[:, :], compare_op=ALU.is_ge, fill=MASKED, base=0,
                            pattern=[[-1, P]], channel_multiplier=1).then_inc(q["mask_ok"], 1)
            pool.wait_ge(q["id0"], 1)
            g.affine_select(out=ident[:, :], in_=ident[:, :], compare_op=ALU.not_equal, fill=1.0, base=0,
                            pattern=[[-1, P]], channel_multiplier=1).then_inc(q["id_ok"], 1)
            g.memset(bd_aug[:, :], 0.0).then_inc(q["bd0"], 1)
            pool.wait_ge(q["bd0"], 1)
            g.memset(bd_aug[R:R + 1, :], 1.0).then_inc(q["bd0"], 1)
            pool.wait_ge(q["bd0"], 2)
            g.memset(raw(dsel[:, :, :, :]), 0.0).then_inc(q["dpad_ok"], 1)
            pool.wait_ge(q["dpad_ok"], 1)
            pool.wait_ge(bias_in, 32)
            g.tensor_tensor(row_bias[R:R + 1, :, :], row_bias[R:R + 1, :, :],
                            base_row[R:R + 1, :].rearrange("p (a d) -> p a d", a=1).broadcast_to((1, E, D)),
                            ALU.add).then_inc(q["bias_ok"], 1)
            pool.wait_ge(q["bias_ok"], 1)
            x_lo(1)
            rstd1(0)

            for i in range(0, B + 2):
                if 1 <= i <= B:
                    rstd2(i - 1)
                    normalize(i - 1)
                if i + 2 < B:
                    x_lo(i + 2)
                if 2 <= i < B:
                    h_lo(i - 2)
                if i + 2 < B:
                    if i % 2 == 1:
                        rstd1(i + 1)
                    c_lo(i + 2)
                if i == 0:
                    pool.wait_ge(q["wb_hi"], 1)
                    sub_lo(wbs[LO][:, :, :], wb_sb[:, :, :], wbs[HI][:, :, :], q["wb_lo"])

        @block.scalar
        def _(act):
            a = nc.scalar

            def copy_hi(hi, src, done):
                a.activation(hi, src, ACT.Copy).then_inc(done, 1)

            def x_hi(b):
                act.wait_ge(xT_in[b], 16)
                if b >= 2:
                    act.wait_ge(q["t_ready"], b - 1)
                copy_hi(xs[:, b % 2, HI, :, :], xT_sb[:, b, :, :], q["x_hi"])

            def c_hi(b):
                act.wait_ge(cT_in[b], 16)
                if b >= 2:
                    act.wait_ge(q["s_ready"], b - 1)
                copy_hi(cs[:, b % 2, HI, :, :], cT_sb[:, b, :, :], q["c_hi"])

            def t_hi(b):
                act.wait_ge(q["t_ready"], b + 1)
                copy_hi(ts[:, HI, :, :], t_ps, q["t_hi"])

            def v_hi(b):
                act.wait_ge(q["v_ready"], b + 1)
                if b >= 2:
                    act.wait_ge(q["o_ready"], b - 1)
                copy_hi(vs[:, b % 2, HI, :, :], v_ps, q["v_hi"])

            def exps(b):
                act.wait_ge(q["nmax_ok"], b + 1)
                if b >= 1:
                    act.wait_ge(q["pt_ready"], b)
                a.activation(prob[:, 0:P], ps_s[:, 0:P], ACT.Exp, bias=nmax[:, b, 0:1], scale=rs1[:, b, 0:1],
                             accum_out=rsum[:, b, 0:1]).then_inc(q["exp_ok"], 1)
                a.activation(prob[:, P:SC], ps_s[:, P:SC], ACT.Exp, bias=nmax[:, b, 1:2], scale=rs1[:, b, 1:2],
                             accum_out=rsum[:, b, 1:2]).then_inc(q["exp_ok"], 1)

            def pt_hi(b):
                act.wait_ge(q["pt_ready"], b + 1)
                if b >= 1:
                    act.wait_ge(q["o_ready"], b)
                copy_hi(pts[:, HI, :], ps_s[:, 0:SC], q["pt_hi"])

            def select_down(b):
                act.wait_ge(q["pick_ok"], b + 1)
                e = act.value_load(pick[0:1, b, 0:1], min_val=0, max_val=E - 1)
                if b == 0:
                    act.wait_ge(q["dw_lo"], 1)
                    act.wait_ge(q["bd_ok"], 16)
                    act.wait_ge(q["dpad_ok"], 1)
                else:
                    act.wait_ge(q["h_ready"], b)
                a.activation(dsel[:, :, :, 0:R], raw(dws[:, bass.ds(e, 1), :, :, :]), ACT.Copy).then_inc(q["dsel_ok"], 1)
                return e

            def relu(b, e):
                act.wait_ge(q["h_ready"], b + 1)
                if b >= 1:
                    act.wait_ge(q["h_lo"], b)
                a.activation(h_f[:, :], h_ps, ACT.Relu, bias=bd_aug[:, bass.ds(e, 1)]).then_inc(q["relu_ok"], 1)
                if b >= 1:
                    act.wait_ge(q["y_ready"], b)
                a.activation(hs[:, HI, :], h_ps, ACT.Relu, bias=bd_aug[:, bass.ds(e, 1)]).then_inc(q["h_hi"], 1)

            def z_hi(b):
                act.wait_ge(q["z_ready"], b + 1)
                if b >= 2:
                    act.wait_ge(q["h_ready"], b - 1)
                for k in range(KD):
                    a.activation(zs[:, b % 2, HI, k, :], z_ps[:, k, :], ACT.Copy,
                                 accum_out=pooled[:, b, k:k + 1]).then_inc(q["z_hi"], 1)

            def z_squares(b):
                act.wait_ge(q["z_lo"], b + 1)
                for k in range(KD):
                    if b + k >= 1:
                        act.wait_ge(q["z_sq"], KD * b + k)
                    a.activation(sq[:, :], z_ps[:, k, :], ACT.Square,
                                 accum_out=pooled[:, b, KD + k:KD + k + 1]).then_inc(q["z_sq"], 1)

            def u_hi(j):
                act.wait_ge(q["u_sum"], j + 1)
                copy_hi(us[:, 2 * j:2 * j + 2, HI, :], u_f[:, j % 2, :, :], q["u_hi"])

            act.dma_start(mu_sb[:, :, :], mu_T.rearrange("(k p) e -> p k e", p=P)).then_inc(disc_in, 16)
            act.dma_start(sg_sb[:, :, :], sigma_T.rearrange("(k p) e -> p k e", p=P)).then_inc(disc_in, 16)
            act.dma_start(base_row[R:R + 1, :], base_b.rearrange("(a d) -> a d", a=1)).then_inc(bias_in, 16)
            act.wait_ge(q["bias0"], 1)
            act.dma_start(row_bias[R:R + 1, :, :], conv_b.rearrange("(a e) d -> a e d", a=1)).then_inc(bias_in, 16)
            c_hi(0)
            act.wait_ge(wv_in, 16)
            copy_hi(wvs[HI][:, :, :], wv_sb[:, :, :], q["wv_hi"])
            x_hi(0)
            act.wait_ge(q["mc_ready"], 1)
            copy_hi(mc[HI][:, :, :], t_ps, q["mc_hi"])
            c_hi(1)
            v_hi(0)
            x_hi(1)
            t_hi(0)
            v_hi(1)
            for i in range(0, B + 2):
                if i >= 2:
                    e = select_down(i - 2)
                if i + 2 < B:
                    x_hi(i + 2)
                if i < B:
                    exps(i)
                if i + 1 < B:
                    t_hi(i + 1)
                if i < B:
                    pt_hi(i)
                if i == B:
                    relu(i - 2, e)
                if 1 <= i <= B:
                    z_hi(i - 1)
                if i >= 2 and i != B:
                    relu(i - 2, e)
                if 1 <= i <= B:
                    z_squares(i - 1)
                if i + 2 < B:
                    c_hi(i + 2)
                if i == 1:
                    u_hi(3)
                if 1 <= i and i + 1 < B:
                    v_hi(i + 1)
                if i == 0:
                    u_hi(0)
                    act.wait_ge(wb_in, 16)
                    copy_hi(wbs[HI][:, :, :], wb_sb[:, :, :], q["wb_hi"])
                    u_hi(1)
                    act.wait_ge(down_in, 16)
                    copy_hi(dws[:, :, HI, :, :], dw_sb[:, :, :, :], q["dw_hi"])
                    u_hi(2)

        @block.vector
        def _(dve):
            v = nc.vector

            def sub_lo(lo, src, hi, done):
                v.tensor_tensor(lo, src, raw(hi), ALU.subtract).then_inc(done, 1)

            def moments(src, stats, mom, b, st_ok, mom_ok):
                for t in range(QT):
                    v.bn_stats(stats[:, b % 2, t, :], src[:, b, t, :]).then_inc(st_ok, 1)
                for t in range(QT):
                    dve.wait_ge(st_ok, QT * b + t + 1)
                    v.bn_aggr(mom[:, b, t, :], stats[:, b % 2, t, :]).then_inc(mom_ok, 1)

            def moments1(b):
                dve.wait_ge(x_in[b], 16)
                if b >= 2:
                    dve.wait_ge(q["mom1_ok"], QT * (b - 1))
                moments(x_sb, stats1, mom1, b, q["st1_ok"], q["mom1_ok"])

            def argmin(b):
                dve.wait_ge(q["l_ready"], b + 1)
                v.tensor_tensor(nloss[:, b, :], l_ps, loss_c[:, :], ALU.add).then_inc(q["nloss_ok"], 1)
                dve.wait_ge(q["nloss_ok"], b + 1)
                v.max(best[:, b, :], nloss[:, b, :]).then_inc(q["best_ok"], 1)
                dve.wait_ge(q["best_ok"], b + 1)
                v.max_index(pick[:, b, :], best[:, b, :], nloss[:, b, :]).then_inc(q["pick_ok"], 1)

            def row_max(b):
                dve.wait_ge(q["s_ready"], b + 1)
                v.reduce_max(rmax[:, b, 0:1], ps_s[:, 0:P], AX.X).then_inc(q["max_ok"], 1)
                v.reduce_max(rmax[:, b, 1:2], ps_s[:, P:SC], AX.X).then_inc(q["max_ok"], 1)
                dve.wait_ge(q["max_ok"], QT * (b + 1))
                dve.wait_ge(q["rs1_ok"], b // 2 + 1)
                v.scalar_tensor_tensor(out=nmax[:, b, :], in0=rmax[:, b, :], scalar=-1.0, in1=rs1[:, b, :],
                                       op0=ALU.mult, op1=ALU.mult).then_inc(q["nmax_ok"], 1)

            def normalize_last():
                b, t = B - 1, QT - 1
                dve.wait_ge(q["nm2_ok"], b + 1)
                dve.wait_ge(q["z_ready"], b)
                v.tensor_scalar(z[:, t, :], x2[:, b, t, :], rs2[:, b, t:t + 1], nm2[:, b, t:t + 1],
                                ALU.mult, ALU.add).then_inc(q["z_ok"], 1)

            def t_lo(b):
                dve.wait_ge(q["t_hi"], b + 1)
                sub_lo(ts[:, LO, :, :], t_ps, ts[:, HI, :, :], q["t_lo"])

            def v_lo(b):
                dve.wait_ge(q["v_hi"], b + 1)
                sub_lo(vs[:, b % 2, LO, :, :], v_ps, vs[:, b % 2, HI, :, :], q["v_lo"])

            def pt_lo(b):
                dve.wait_ge(q["pt_hi"], b + 1)
                sub_lo(pts[:, LO, :], ps_s[:, 0:SC], pts[:, HI, :], q["pt_lo"])

            def z_lo(b):
                dve.wait_ge(q["z_hi"], KD * (b + 1))
                sub_lo(zs[:, b % 2, LO, :, :], z_ps, zs[:, b % 2, HI, :, :], q["z_lo"])

            def h_lo(b):
                dve.wait_ge(q["relu_ok"], b + 1)
                dve.wait_ge(q["h_hi"], b + 1)
                sub_lo(hs[:, LO, :], h_f[:, :], hs[:, HI, :], q["h_lo"])

            def residual(b):
                dve.wait_ge(q["exp_ok"], QT * (b + 1))
                v.reciprocal(rinv[:, b, :], rsum[:, b, :]).then_inc(q["rinv_ok"], 1)
                dve.wait_ge(q["rinv_ok"], b + 1)
                dve.wait_ge(q["o_ready"], b + 1)
                for t in range(QT):
                    v.scalar_tensor_tensor(out=x2[:, b, t, :], in0=o_ps[:, t, :], scalar=rinv[:, b, t:t + 1],
                                           in1=x_sb[:, b, t, :], op0=ALU.mult, op1=ALU.add).then_inc(q["x2_ok"], 1)

            def moments2(b):
                dve.wait_ge(q["x2_ok"], QT * (b + 1))
                if b >= 2:
                    dve.wait_ge(q["mom2_ok"], QT * (b - 1))
                moments(x2, stats2, mom2, b, q["st2_ok"], q["mom2_ok"])

            def finish(b):
                dve.wait_ge(q["y_ready"], b + 1)
                dve.wait_ge(q["z_ok"], QT * (b + 1))
                v.tensor_tensor(x2[:, b, :, :], y_ps[b % 2], x2[:, b, :, :], ALU.add).then_inc(q["fin_ok"], 1)

            def fold_sum(j):
                dve.wait_ge(q["u_ready"], j + 1)
                if j >= 2:
                    dve.wait_ge(q["u_lo"], j - 1)
                bank = fold_bank[j % FB][:, :].rearrange("p (e d) -> p e d", e=2)
                v.tensor_tensor(u_f[:, j % 2, :, :], bank, row_bias[:, 2 * j:2 * j + 2, :], ALU.add).then_inc(q["u_sum"], 1)

            def fold_lo(j):
                dve.wait_ge(q["u_hi"], j + 1)
                sub_lo(us[:, 2 * j:2 * j + 2, LO, :], u_f[:, j % 2, :, :], us[:, 2 * j:2 * j + 2, HI, :], q["u_lo"])

            def discriminator():
                dve.wait_ge(disc_in, 32)
                v.tensor_tensor(sg2[:, :, :], sg_sb[:, :, :], sg_sb[:, :, :], ALU.mult).then_inc(q["sg2_ok"], 1)
                dve.wait_ge(q["sg2_ok"], 1)
                v.reciprocal(inv_var[:, :, :], sg2[:, :, :]).then_inc(q["iv_ok"], 1)
                dve.wait_ge(q["iv_ok"], 1)
                v.tensor_tensor(mu_iv[:, :, :], mu_sb[:, :, :], inv_var[:, :, :], ALU.mult).then_inc(q["muiv_ok"], 1)
                dve.wait_ge(q["muiv_ok"], 1)
                v.tensor_scalar(tab_m2[:, :, :], inv_var[:, :, :], -1.0 / S, None, ALU.mult).then_inc(q["tab_ok"], 1)
                v.tensor_scalar(tab_m1[:, :, :], mu_iv[:, :, :], 2.0 / S, None, ALU.mult).then_inc(q["tab_ok"], 1)
                v.scalar_tensor_tensor(out=tab_c[:, :, :], in0=mu_iv[:, :, :], scalar=-1.0, in1=mu_sb[:, :, :],
                                       op0=ALU.mult, op1=ALU.mult).then_inc(q["tab_ok"], 1)

            v.memset(ones_col[:, :], 1.0).then_inc(q["ones_ok"], 1)
            v.memset(warm[:, :], 0.0).then_inc(q["warm_ok"], 1)
            dve.wait_ge(wq_in, 16)
            v.reduce_sum(wq_sum[:, :], wqT_sb[:, :, :], AX.X).then_inc(q["wq_summed"], 1)
            dve.wait_ge(q["wq_summed"], 1)
            v.tensor_scalar(wq_sum[:, :], wq_sum[:, :], 1.0 / D, None, ALU.mult).then_inc(q["wq_meaned"], 1)
            dve.wait_ge(q["wq_meaned"], 1)
            for k in range(KD):
                v.tensor_scalar(wqc[:, k, :], wqT_sb[:, k, :], wq_sum[:, k:k + 1], None,
                                ALU.subtract).then_inc(q["wqc_ok"], 1)
            def c_lo(b):
                dve.wait_ge(q["c_hi"], b + 1)
                sub_lo(cs[:, b % 2, LO, :, :], cT_sb[:, b, :, :], cs[:, b % 2, HI, :, :], q["c_lo"])

            c_lo(0)
            dve.wait_ge(q["wv_hi"], 1)
            sub_lo(wvs[LO][:, :, :], wv_sb[:, :, :], wvs[HI][:, :, :], q["wv_lo"])
            dve.wait_ge(q["x_hi"], 1)
            sub_lo(xs[:, 0, LO, :, :], xT_sb[:, 0, :, :], xs[:, 0, HI, :, :], q["x_lo"])
            discriminator()
            dve.wait_ge(q["mc_hi"], 1)
            sub_lo(mc[LO][:, :, :], t_ps, mc[HI][:, :, :], q["mc_lo"])
            v_lo(0)
            c_lo(1)
            t_lo(0)
            moments1(0)
            moments1(1)
            v_lo(1)
            dve.wait_ge(q["lossc_ready"], 1)
            v.tensor_copy(loss_c[:, :], ps_o[0:1, 0:E]).then_inc(q["lossc_ok"], 1)
            dve.wait_ge(q["lossc_ok"], 1)
            for i in range(0, B + 2):
                if i < B:
                    row_max(i)
                if 3 <= i <= B:
                    finish(i - 3)
                if i == 1:
                    dve.wait_ge(q["dw_hi"], 1)
                    sub_lo(dws[:, :, LO, :, :], dw_sb[:, :, :, :], dws[:, :, HI, :, :], q["dw_lo"])
                if i == 2:
                    fold_lo(2)
                    fold_lo(3)
                if i == B:
                    normalize_last()
                if i + 1 < B:
                    t_lo(i + 1)
                if i < B:
                    pt_lo(i)
                if i == 0:
                    fold_sum(0)
                if i >= B:
                    h_lo(i - 2)
                if 1 <= i <= B:
                    z_lo(i - 1)
                if i + 2 < B:
                    moments1(i + 2)
                if i == B:
                    finish(B - 2)
                if i == 1:
                    fold_sum(3)
                if i < B:
                    residual(i)
                    moments2(i)
                if i == 0:
                    fold_lo(0)
                    fold_sum(1)
                    fold_lo(1)
                    fold_sum(2)
                if 1 <= i <= B:
                    argmin(i - 1)
                if 1 <= i and i + 1 < B:
                    v_lo(i + 1)
            finish(B - 1)

        @block.tensor
        def _(pe):
            t = nc.tensor

            def mm(dst, lhsT, rhs, start, stop):
                return t.matmul(dst, lhsT, rhs, start=start, stop=stop, skip_group_check=True)

            def mm_split(dst, lhs, rhs, start, stop):
                mm(dst, lhs[LO], rhs[HI], start, False)
                mm(dst, lhs[HI], rhs[LO], False, False)
                return mm(dst, lhs[HI], rhs[HI], False, stop)

            def halves(tile, *at):
                return [tile[(slice(None),) + at[:-1] + (h,) + tuple(at[-1])] for h in (HI, LO)]

            def project_t(b):
                pe.wait_ge(q["x_lo"], b + 1)
                if b == 0:
                    pe.wait_ge(q["mc_lo"], 1)
                else:
                    pe.wait_ge(q["t_lo"], b)
                for m in range(KD):
                    for k in range(KD):
                        last = mm_split(t_ps[:, m, :], [mc[h][:, k, m * P:(m + 1) * P] for h in (HI, LO)],
                                        [xs[:, b % 2, h, k, :] for h in (HI, LO)], k == 0, k == KD - 1)
                last.then_inc(q["t_ready"], 1)

            def project_v(b):
                pe.wait_ge(q["c_lo"], b + 1)
                if b == 0:
                    pe.wait_ge(q["wv_lo"], 1)
                else:
                    pe.wait_ge(q["v_lo"], b)
                for m in range(QT):
                    for k in range(KD):
                        last = mm_split(v_ps[:, m, :], [cs[:, b % 2, h, k, m * P:(m + 1) * P] for h in (HI, LO)],
                                        [wvs[h][:, k, :] for h in (HI, LO)], k == 0, k == KD - 1)
                last.then_inc(q["v_ready"], 1)

            def scores(b):
                pe.wait_ge(q["t_lo"], b + 1)
                pe.wait_ge(q["c_lo"], b + 1)
                if b == 0:
                    pe.wait_ge(q["idh_ok"], 1)
                    pe.wait_ge(q["mask_ok"], 1)
                else:
                    pe.wait_ge(q["pt_lo"], b)
                for m in range(QT):
                    lo = 0 if m == 0 else P
                    keys = (m + 1) * P
                    dst = ps_s[:, lo:lo + keys]
                    for k in range(KD):
                        mm_split(dst, [ts[:, h, k, m * P:(m + 1) * P] for h in (HI, LO)],
                                 [cs[:, b % 2, h, k, 0:keys] for h in (HI, LO)], k == 0, False)
                    last = mm(ps_s[:, lo + keys - P:lo + keys], ident_h[:, :], mask_h[:, :], False, True)
                last.then_inc(q["s_ready"], 1)

            def transpose_p(b):
                pe.wait_ge(q["exp_ok"], QT * (b + 1))
                if b == 0:
                    pe.wait_ge(q["id_ok"], 1)
                for j in range(SC // P):
                    last = t.transpose(ps_s[:, j * P:(j + 1) * P], prob[:, j * P:(j + 1) * P], ident[:, :])
                last.then_inc(q["pt_ready"], 1)

            def attend(b):
                pe.wait_ge(q["pt_lo"], b + 1)
                pe.wait_ge(q["v_lo"], b + 1)
                if b >= 1:
                    pe.wait_ge(q["x2_ok"], QT * b)
                for m, j, k, first, stop in ((0, 0, 0, True, True), (1, 1, 0, True, False), (1, 2, 1, False, True)):
                    last = mm_split(o_ps[:, m, :], [pts[:, h, j * P:(j + 1) * P] for h in (HI, LO)],
                                    [vs[:, b % 2, h, k, :] for h in (HI, LO)], first, stop)
                last.then_inc(q["o_ready"], 1)

            def transpose_z(b):
                pe.wait_ge(q["z_ok"], QT * (b + 1))
                if b >= 1:
                    pe.wait_ge(q["z_sq"], KD * b)
                for k in range(KD):
                    for m in range(QT):
                        last = t.transpose(z_ps[:, k, m * P:(m + 1) * P], z[:, m, k * P:(k + 1) * P], ident[:, :])
                last.then_inc(q["z_ready"], 1)

            def base(b):
                pe.wait_ge(q["z_lo"], b + 1)
                if b == 0:
                    pe.wait_ge(q["wb_lo"], 1)
                    pe.wait_ge(q["u_sum"], FB)
                if b >= 2:
                    pe.wait_ge(q["fin_ok"], b - 1)
                for m in range(QT):
                    for k in range(KD):
                        mm_split(y_ps[b % 2][:, m, :],
                                 [zs[:, b % 2, h, k, m * P:(m + 1) * P] for h in (HI, LO)],
                                 [wbs[h][:, k, :] for h in (HI, LO)], m == 0 and k == 0, False)

            def losses(b):
                pe.wait_ge(q["z_sq"], KD * (b + 1))
                if b == 0:
                    pe.wait_ge(q["u_sum"], E // 2)
                else:
                    pe.wait_ge(q["nloss_ok"], b)
                    pe.wait_ge(q["h_hi"], b)
                tabs = [tab_m1, tab_m2]
                for j in range(2 * KD):
                    last = mm(l_ps, pooled[:, b, j:j + 1], tabs[j // KD][:, j % KD, :], j == 0, j == 2 * KD - 1)
                last.then_inc(q["l_ready"], 1)

            def down(b):
                pe.wait_ge(q["dsel_ok"], b + 1)
                pe.wait_ge(q["nloss_ok"], b + 1)
                for k in range(KD):
                    last = mm_split(h_ps, [dsel[:, h, k, :] for h in (HI, LO)],
                                    [zs[:, b % 2, h, k, :] for h in (HI, LO)], k == 0, k == KD - 1)
                last.then_inc(q["h_ready"], 1)

            def chosen(b):
                pe.wait_ge(q["pick_ok"], b + 1)
                return pe.value_load(pick[0:1, b, 0:1], min_val=0, max_val=E - 1)

            def expert(b, e):
                pe.wait_ge(q["h_lo"], b + 1)
                if b == 0:
                    pe.wait_ge(q["u_lo"], E // 2)
                for m in range(QT):
                    last = mm_split(y_ps[b % 2][:, m, :], [hs[:, h, m * P:(m + 1) * P] for h in (HI, LO)],
                                    [us[:, bass.ds(e, 1), h, :] for h in (HI, LO)], False, m == QT - 1)
                last.then_inc(q["y_ready"], 1)

            def fold(j, parts=(0, 1)):
                pe.wait_ge(up_in[j // 2], 16)
                pe.wait_ge(conv_in[j], 16)
                if j >= FB:
                    pe.wait_ge(q["u_sum"], j - FB + 1)
                bank = fold_bank[j % FB]
                for s in parts:
                    for k in range(KD):
                        last = mm(bank[:, s * D:(s + 1) * D], up_sb[:, 2 * j + s, k, :], cw_sb[:, 2 * j + s, k, :],
                                  k == 0, k == KD - 1)
                if s == 1:
                    last.then_inc(q["u_ready"], 1)

            pe.wait_ge(q["warm_ok"], 1)
            for _ in range(WARM):
                mm(ps_y[1][:, :], warm[:, 0:P], warm[:, :], True, True)
            pe.wait_ge(wk_in, 16)
            pe.wait_ge(q["wqc_ok"], KD)
            for m in range(KD):
                for k in range(KD):
                    last = mm(t_ps[:, m, :], wqc[:, k, m * P:(m + 1) * P], wkT_sb[:, k, :], k == 0, k == KD - 1)
            last.then_inc(q["mc_ready"], 1)
            project_v(0)
            pe.wait_ge(q["tab_ok"], 3)
            pe.wait_ge(q["ones_ok"], 1)
            for k in range(KD):
                last = mm(ps_o[0:1, 0:E], ones_col[:, :], tab_c[:, k, :], k == 0, k == KD - 1)
            last.then_inc(q["lossc_ready"], 1)
            project_t(0)
            project_v(1)
            for i in range(0, B + 2):
                if i < B:
                    scores(i)
                if i + 1 < B:
                    project_t(i + 1)
                if i == 0:
                    fold(0, (0,))
                if i == 1:
                    fold(3)
                if 1 <= i < B:
                    transpose_z(i - 1)
                if i >= 2:
                    down(i - 2)
                if i < B:
                    transpose_p(i)
                if i == 0:
                    fold(0, (1,))
                if 1 <= i and i + 1 < B:
                    project_v(i + 1)
                if i < B:
                    attend(i)
                if i == B:
                    transpose_z(i - 1)
                if i >= B:
                    expert(i - 2, chosen(i - 2))
                if 1 <= i < B:
                    base(i - 1)
                if 1 <= i <= B:
                    losses(i - 1)
                if i == B:
                    base(i - 1)
                if 2 <= i < B:
                    expert(i - 2, chosen(i - 2))
                if i == 0:
                    fold(1)
                    fold(2)


_INS = ["x", "xT", "ctxT", "wqT", "wkT", "wv", "base_wT", "mu_T", "sigma_T",
        "down_w", "down_bT", "up_aug", "conv_wT", "conv_b", "base_b"]


def kernel(**inputs):
    import numpy as _np
    import concourse.bacc as _bacc
    from concourse import mybir as _mybir
    from concourse.bass_utils import run_bass_kernel_spmd as _run

    a = {n: _np.asarray(v) for n, v in inputs.items()}
    laid = {
        "x": a["x"],
        "xT": a["x"].transpose(0, 2, 1),
        "ctxT": a["ctx_1024"].transpose(0, 2, 1),
        "wqT": a["L0_xattn_w_q"].T,
        "wkT": a["L0_xattn_w_k"].T,
        "wv": a["L0_xattn_w_v"],
        "base_wT": a["L0_ffn_base_W"].T,
        "mu_T": a["L0_ffn_disc_mu"].T,
        "sigma_T": a["L0_ffn_disc_sigma"].T,
        "down_w": a["L0_ffn_down_W"],
        "down_bT": a["L0_ffn_down_b"].T,
        "up_aug": _np.concatenate([a["L0_ffn_up_W"].transpose(0, 2, 1), a["L0_ffn_up_b"][:, :, None]], axis=2),
        "conv_wT": a["L0_ffn_conv_W"].transpose(0, 2, 1),
        "conv_b": a["L0_ffn_conv_b"],
        "base_b": a["L0_ffn_base_b"],
    }
    nc = _bacc.Bacc("TRN2", target_bir_lowering=False, num_devices=1)
    arrays, args = {}, []
    for name in _INS:
        arr = _np.ascontiguousarray(laid[name])
        arrays[f"in_{name}"] = arr
        args.append(nc.dram_tensor(f"in_{name}", arr.shape, _mybir.dt.from_np(arr.dtype), kind="ExternalInput").ap())
    out = nc.dram_tensor("out_0", a["x"].shape, _mybir.dt.from_np(a["x"].dtype), kind="ExternalOutput").ap()
    xattn_ffn_program(nc, *args, out)
    r = _run(nc, [arrays], core_ids=[0])
    return r.results[0]["out_0"]
```

```python
import numpy as np
import concourse.bass as bass
from concourse import mybir
from contextlib import ExitStack


def xattn_ffn_program(nc, x, xT, ctxT, wqT, wkT, wv, base_wT, mu_T, sigma_T,
                      down_w, down_bT, up_aug, conv_wT, conv_b, base_b, out):
    f32 = mybir.dt.float32
    f32r = mybir.dt.float32r
    bf16 = mybir.dt.bfloat16
    u32 = mybir.dt.uint32
    ALU = mybir.AluOpType
    ACT = mybir.ActivationFunctionType
    AX = mybir.AxisListType

    P = 128
    B, S, D = x.shape
    E, R = down_bT.shape[1], down_w.shape[3]
    KD = D // P
    QT = S // P
    SC = P * (1 + 2)
    EPS = 1e-5
    MASKED = -1e30
    HI, LO = 0, 1
    WARM = 7

    ctx = ExitStack()
    with ctx:
        def sb(name, shape, dt=f32):
            return ctx.enter_context(nc.sbuf_tensor(name, shape, dt))

        def pb(name, shape=(P, 512)):
            return ctx.enter_context(nc.psum_tensor(name, list(shape), f32))

        def sem(name):
            return ctx.enter_context(nc.semaphore(name))

        x_sb = sb("x_sb", [P, B, QT, D])
        xT_sb = sb("xT_sb", [P, B, KD, S])
        cT_sb = sb("cT_sb", [P, B, KD, S])
        wqT_sb = sb("wqT_sb", [P, KD, D])
        wkT_sb = sb("wkT_sb", [P, KD, D])
        wv_sb = sb("wv_sb", [P, KD, D])
        wb_sb = sb("wb_sb", [P, KD, D])
        mu_sb = sb("mu_sb", [P, KD, E])
        sg_sb = sb("sg_sb", [P, KD, E])
        dw_sb = sb("dw_sb", [P, E, KD, R])
        up_sb = sb("up_sb", [P, E, KD, R + 1])
        cw_sb = sb("cw_sb", [P, E, KD, D])
        row_bias = sb("row_bias", [P, E, D])
        base_row = sb("base_row", [P, D])
        bd_sb = sb("bd_sb", [P, E])
        ident = sb("ident", [P, P])
        ident_h = sb("ident_h", [P, P], bf16)
        mask_h = sb("mask_h", [P, P], bf16)
        half_neg = sb("half_neg", [P, QT])
        ones_col = sb("ones_col", [P, 1])
        warm = sb("warm", [P, 4 * P], bf16)
        wq_sum = sb("wq_sum", [P, KD])
        wqc = sb("wqc", [P, KD, D])
        mc = [sb(f"mc{h}", [P, KD, D], f32r) for h in (HI, LO)]
        wvs = [sb(f"wvs{h}", [P, KD, D], f32r) for h in (HI, LO)]
        wbs = [sb(f"wbs{h}", [P, KD, D], f32r) for h in (HI, LO)]
        dws = sb("dws", [P, E, 2, KD, R], f32r)
        u_f = sb("u_f", [P, 2, 2, D])
        ua = sb("ua", [P, E, D], f32r)
        ub = sb("ub", [P, E, D], f32r)
        sg2 = sb("sg2", [P, KD, E])
        inv_var = sb("inv_var", [P, KD, E])
        mu_iv = sb("mu_iv", [P, KD, E])
        tab_m1 = sb("tab_m1", [P, KD, E])
        tab_m2 = sb("tab_m2", [P, KD, E])
        tab_c = sb("tab_c", [P, KD, E])
        loss_c = sb("loss_c", [1, E])
        xs = sb("xs", [P, 2, 2, KD, S], f32r)
        cs = sb("cs", [P, 2, 2, KD, S], f32r)
        ts = sb("ts", [P, 2, KD, S], f32r)
        vs = sb("vs", [P, 2, 2, QT, D], f32r)
        prob = sb("prob", [P, SC])
        pts = sb("pts", [P, 2, SC], f32r)
        stats1 = sb("stats1", [P, 2, QT, 6])
        mom1 = sb("mom1", [P, B, QT, 2])
        var1 = sb("var1", [P, QT])
        rs1 = sb("rs1", [P, B, QT])
        rmax = sb("rmax", [P, B, QT])
        nmax = sb("nmax", [P, B, QT])
        rsum = sb("rsum", [P, B, QT])
        rinv = sb("rinv", [P, B, QT])
        x2 = x_sb
        stats2 = sb("stats2", [P, 2, QT, 6])
        mom2 = sb("mom2", [P, B, QT, 2])
        var2 = sb("var2", [P, QT])
        negm = sb("negm", [P, QT])
        nm2 = sb("nm2", [P, B, QT])
        rs2 = sb("rs2", [P, B, QT])
        z = sb("z", [P, QT, D])
        zs = sb("zs", [P, 2, 2, KD, S], f32r)
        sq = sb("sq", [P, S])
        pooled = sb("pooled", [P, B, 2 * KD])
        nloss = sb("nloss", [1, B, E])
        best = sb("best", [1, B, 8])
        pick = sb("pick", [1, B, 8], u32)
        dsel = sb("dsel", [P, 2, 2, KD, 2, R], f32r)
        h_f = sb("h_f", [P, 2, S])
        ha = sb("ha", [P, 2, S], f32r)
        hb = sb("hb", [P, 2, S], f32r)

        ps_t, ps_v, ps_s, ps_o, ps_z, ps_h = [pb(n) for n in ("ps_t", "ps_v", "ps_s", "ps_o", "ps_z", "ps_h")]
        ps_y = [pb("ps_y0"), pb("ps_y1")]
        t_ps = ps_t[:, :].rearrange("p (k s) -> p k s", k=KD)
        v_ps = ps_v[:, :].rearrange("p (k s) -> p k s", k=QT)
        o_ps = [[ps_o[:, t * D:(t + 1) * D] for t in range(QT)]] * (B - 1) + [[ps_o[:, 0:D], ps_v[:, 0:D]]]
        z_ps = ps_z[:, :].rearrange("p (k s) -> p k s", k=KD)
        z_ps_last = [ps_z[:, 0:S], ps_t[:, 0:S]]
        h_ps = [ps_h[:, 0:S]] * (B - 1) + [ps_z[:, 0:S]]
        l_ps = [ps_h[0:1, S:S + E]] * (B - 1) + [ps_s[0:1, 0:E]]
        y_ps = [[ps_y[b % 2][:, t * D:(t + 1) * D] for t in range(QT)] for b in range(B)]
        y_ps[B - 2] = [ps_v[:, t * D:(t + 1) * D] for t in range(QT)]
        y_ps[B - 1][QT - 1] = ps_o[:, 0:D]

        fold_bank = [ps_h, ps_y[1], ps_y[0], ps_y[1]]

        wq_in, wk_in = [[sem(f"{n}{k}") for k in range(KD)] for n in ("wq_in", "wk_in")]
        wv_in, wb_in = sem("wv_in"), sem("wb_in")
        disc_in, down_in, bias_in = sem("disc_in"), sem("down_in"), sem("bias_in")
        up_in = [sem(f"up_in{j}") for j in range(2)]
        conv_in = [sem(f"conv_in{j}") for j in range(4)]
        xT_in = [sem(f"xT_in{b}") for b in range(B)]
        cT_in = [sem(f"cT_in{b}") for b in range(B)]
        x_in = [sem(f"x_in{b}") for b in range(B)]
        stored = sem("stored")
        names = ("warm_ok id0 id_ok idh0 idh_ok mask0 mask_ok pow_ok ones_ok hone_ok bd_ok bias0 bias_ok "
                 "wq_summed wq_meaned wqc_ok mc_ready mc_hi mc_lo wv_hi wv_lo wb_hi wb_lo dw_hi dw_lo "
                 "sg2_ok iv_ok muiv_ok tab_ok lossc_ready lossc_ok u_ready u_sum u_hi u_lo u_row u_twice "
                 "x_hi x_lo c_hi c_lo t_ready t_hi t_lo v_ready v_hi v_lo st1_ok mom1_ok var1_ok rs1_ok "
                 "s_ready max_ok nmax_ok exp_ok pt_ready pt_hi pt_lo o_ready rinv_ok x2_ok st2_ok mom2_ok "
                 "var2_ok negm_ok rs2_ok nm2_ok z_ok z_ready z_hi z_sq z_lo l_ready nloss_ok best_ok pick_ok dsel_ok "
                 "h_ready h_hi relu_ok hb_ok h_lo y_ready fin_ok").split()
        q = {n: sem(n) for n in names}

        def raw(ap):
            return ap.bitcast(f32)

        block = ctx.enter_context(nc.Block())

        @block.sync
        def _(sp):
            def weights(dst, src, done):
                sp.dma_start(dst[:, :, :], src.rearrange("(k p) n -> p k n", p=P)).then_inc(done, 16)

            def transposed(dst, src, b, done):
                sp.dma_start(dst[:, b, :, :], src[b].rearrange("(k p) s -> p k s", p=P)).then_inc(done[b], 16)

            def natural(b):
                sp.dma_start(x_sb[:, b, :, :], x[b].rearrange("(t p) d -> p t d", p=P)).then_inc(x_in[b], 16)

            def batch(b):
                transposed(xT_sb, xT, b, xT_in)
                transposed(cT_sb, ctxT, b, cT_in)
                natural(b)

            def fold_weights(j):
                es = slice(4 * j, 4 * j + 4)
                sp.dma_start(up_sb[:, es, :, :], up_aug[:, es, :, :]).then_inc(up_in[j], 16)
                for i in (2 * j, 2 * j + 1):
                    sp.dma_start(cw_sb[:, 2 * i:2 * i + 2, :, :],
                                 conv_wT[2 * i:2 * i + 2].rearrange("e (k p) o -> p e k o", p=P)).then_inc(conv_in[i], 16)

            for k in range(KD):
                sp.dma_start(wqT_sb[:, k, :], wqT[k * P:(k + 1) * P, :]).then_inc(wq_in[k], 16)
            transposed(cT_sb, ctxT, 0, cT_in)
            weights(wv_sb, wv, wv_in)
            transposed(xT_sb, xT, 0, xT_in)
            transposed(cT_sb, ctxT, 1, cT_in)
            sp.dma_start(base_row[R:R + 1, :], base_b.rearrange("(a d) -> a d", a=1)).then_inc(bias_in, 16)
            sp.wait_ge(q["bias0"], 1)
            sp.dma_start(row_bias[R:R + 1, :, :], conv_b.rearrange("(a e) d -> a e d", a=1)).then_inc(bias_in, 16)
            natural(0)
            sp.dma_start(mu_sb[:, :, :], mu_T.rearrange("(k p) e -> p k e", p=P)).then_inc(disc_in, 16)
            sp.dma_start(sg_sb[:, :, :], sigma_T.rearrange("(k p) e -> p k e", p=P)).then_inc(disc_in, 16)
            transposed(xT_sb, xT, 1, xT_in)
            natural(1)
            fold_weights(0)
            weights(wb_sb, base_wT, wb_in)
            batch(2)
            fold_weights(1)
            sp.dma_start(dw_sb[:, :, :, :], down_w).then_inc(down_in, 16)
            for half in range(2):
                sp.dma_start(bd_sb[half * R:(half + 1) * R, :], down_bT).then_inc(q["bd_ok"], 16)
            for b in range(3, B):
                batch(b)
            sp.wait_ge(q["u_hi"], E // 2)
            sp.wait_ge(q["u_lo"], E // 2)
            sp.dma_start(raw(ub[R + 1:R + 2, :, :]), raw(ua[R:R + 1, :, :])).then_inc(q["u_row"], 16)
            sp.wait_ge(q["u_row"], 16)
            sp.dma_start(raw(ua[R:2 * R, :, :]), raw(ua[0:R, :, :])).then_inc(q["u_twice"], 16)
            for b in range(B - 1):
                sp.wait_ge(q["fin_ok"], b + 1)
                sp.dma_start(out[b].rearrange("(t p) d -> p t d", p=P), x2[:, b, :, :]).then_inc(stored, 16)
            for t in range(QT):
                sp.wait_ge(q["fin_ok"], B + t)
                sp.dma_start(out[B - 1, t * P:(t + 1) * P, :], x2[:, B - 1, t, :]).then_inc(stored, 16)
            sp.wait_ge(stored, 16 * (B - 1 + QT))

        @block.gpsimd
        def _(pool):
            g = nc.gpsimd

            def sub_lo(lo, src, hi, done):
                g.tensor_tensor(lo, src, raw(hi), ALU.subtract).then_inc(done, 1)

            def x_lo(b):
                pool.wait_ge(q["x_hi"], b + 1)
                sub_lo(xs[:, b % 2, LO, :, :], xT_sb[:, b, :, :], xs[:, b % 2, HI, :, :], q["x_lo"])

            def c_lo(b):
                pool.wait_ge(q["c_hi"], b + 1)
                sub_lo(cs[:, b % 2, LO, :, :], cT_sb[:, b, :, :], cs[:, b % 2, HI, :, :], q["c_lo"])

            def rstd1(b):
                pool.wait_ge(q["mom1_ok"], QT * (b + 1))
                if b >= 1:
                    pool.wait_ge(q["rs1_ok"], b)
                g.tensor_scalar(var1[:, :], mom1[:, b, :, 1], float(D), EPS * D, ALU.mult, ALU.add).then_inc(q["var1_ok"], 1)
                pool.wait_ge(q["var1_ok"], b + 1)
                g.tensor_tensor(rs1[:, b, :], var1[:, :], half_neg[:, :], ALU.pow).then_inc(q["rs1_ok"], 1)

            def rstd2(b):
                pool.wait_ge(q["mom2_ok"], QT * (b + 1))
                if b >= 1:
                    pool.wait_ge(q["rs2_ok"], b)
                    pool.wait_ge(q["nm2_ok"], b)
                g.tensor_scalar(var2[:, :], mom2[:, b, :, 1], 1.0, EPS, ALU.mult, ALU.add).then_inc(q["var2_ok"], 1)
                if b < B - 1:
                    g.tensor_scalar(negm[:, :], mom2[:, b, :, 0], -1.0, 0.0, ALU.mult, ALU.add).then_inc(q["negm_ok"], 1)
                pool.wait_ge(q["var2_ok"], b + 1)
                g.tensor_tensor(rs2[:, b, :], var2[:, :], half_neg[:, :], ALU.pow).then_inc(q["rs2_ok"], 1)
                if b < B - 1:
                    pool.wait_ge(q["rs2_ok"], b + 1)
                    pool.wait_ge(q["negm_ok"], b + 1)
                    g.tensor_tensor(nm2[:, b, :], negm[:, :], rs2[:, b, :], ALU.mult).then_inc(q["nm2_ok"], 1)

            def normalize(b):
                pool.wait_ge(q["nm2_ok"], b + 1)
                pool.wait_ge(q["x2_ok"], QT * (b + 1))
                if b >= 1:
                    pool.wait_ge(q["z_ready"], b)
                for t in range(QT):
                    g.tensor_scalar(z[:, t, :], x2[:, b, t, :], rs2[:, b, t:t + 1], nm2[:, b, t:t + 1],
                                    ALU.mult, ALU.add).then_inc(q["z_ok"], 1)

            g.memset(row_bias[:, :, :], 0.0).then_inc(q["bias0"], 1)
            g.memset(half_neg[:, :], -0.5).then_inc(q["pow_ok"], 1)
            g.memset(ident_h[:, :], 0.0).then_inc(q["idh0"], 1)
            g.memset(mask_h[:, :], 0.0).then_inc(q["mask0"], 1)
            g.memset(ident[:, :], 0.0).then_inc(q["id0"], 1)
            pool.wait_ge(q["idh0"], 1)
            g.affine_select(out=ident_h[:, :], in_=ident_h[:, :], compare_op=ALU.not_equal, fill=1.0, base=0,
                            pattern=[[-1, P]], channel_multiplier=1).then_inc(q["idh_ok"], 1)
            pool.wait_ge(q["mask0"], 1)
            g.affine_select(out=mask_h[:, :], in_=mask_h[:, :], compare_op=ALU.is_ge, fill=MASKED, base=0,
                            pattern=[[-1, P]], channel_multiplier=1).then_inc(q["mask_ok"], 1)
            pool.wait_ge(q["id0"], 1)
            g.affine_select(out=ident[:, :], in_=ident[:, :], compare_op=ALU.not_equal, fill=1.0, base=0,
                            pattern=[[-1, P]], channel_multiplier=1).then_inc(q["id_ok"], 1)
            pool.wait_ge(bias_in, 32)
            for done in ("pow_ok", "idh_ok", "mask_ok", "id_ok"):
                pool.wait_ge(q[done], 1)
            g.tensor_tensor(row_bias[R:R + 1, :, :], row_bias[R:R + 1, :, :],
                            base_row[R:R + 1, :].rearrange("p (a d) -> p a d", a=1).broadcast_to((1, E, D)),
                            ALU.add).then_inc(q["bias_ok"], 1)
            pool.wait_ge(q["bias_ok"], 1)
            x_lo(1)
            rstd1(0)

            for i in range(0, B - 1):
                if i >= 1:
                    rstd2(i - 1)
                    normalize(i - 1)
                if i in (2, 3):
                    c_lo(i + 1)
                rstd1(i + 1)
                if i + 2 < B:
                    x_lo(i + 2)
                    if i not in (1, 2):
                        c_lo(i + 2)
                if i == 0:
                    pool.wait_ge(q["wb_hi"], 1)
                    sub_lo(wbs[LO][:, :, :], wb_sb[:, :, :], wbs[HI][:, :, :], q["wb_lo"])
            L = B - 1
            rstd2(L - 1)
            normalize(L - 1)
            rstd2(L)

        @block.scalar
        def _(act):
            a = nc.scalar

            def copy_hi(hi, src, done):
                a.activation(hi, src, ACT.Copy).then_inc(done, 1)

            def x_hi(b):
                act.wait_ge(xT_in[b], 16)
                if b >= 2:
                    act.wait_ge(q["t_ready"], b - 1)
                copy_hi(xs[:, b % 2, HI, :, :], xT_sb[:, b, :, :], q["x_hi"])

            def c_hi(b):
                act.wait_ge(cT_in[b], 16)
                if b >= 2:
                    act.wait_ge(q["s_ready"], b - 1)
                copy_hi(cs[:, b % 2, HI, :, :], cT_sb[:, b, :, :], q["c_hi"])

            def t_hi(b):
                act.wait_ge(q["t_ready"], b + 1)
                copy_hi(ts[:, HI, :, :], t_ps, q["t_hi"])

            def v_hi(b):
                act.wait_ge(q["v_ready"], b + 1)
                if b >= 2:
                    act.wait_ge(q["o_ready"], b - 1)
                copy_hi(vs[:, b % 2, HI, :, :], v_ps, q["v_hi"])

            def exps(b):
                act.wait_ge(q["nmax_ok"], b + 1)
                if b >= 1:
                    act.wait_ge(q["pt_ready"], b)
                a.activation(prob[:, 0:P], ps_s[:, 0:P], ACT.Exp, bias=nmax[:, b, 0:1], scale=rs1[:, b, 0:1],
                             accum_out=rsum[:, b, 0:1]).then_inc(q["exp_ok"], 1)
                a.activation(prob[:, P:SC], ps_s[:, P:SC], ACT.Exp, bias=nmax[:, b, 1:2], scale=rs1[:, b, 1:2],
                             accum_out=rsum[:, b, 1:2]).then_inc(q["exp_ok"], 1)

            def pt_hi(b):
                act.wait_ge(q["pt_ready"], b + 1)
                if b >= 1:
                    act.wait_ge(q["o_ready"], b)
                copy_hi(pts[:, HI, :], ps_s[:, 0:SC], q["pt_hi"])

            def chosen(b):
                act.wait_ge(q["pick_ok"], b + 1)
                return act.value_load(pick[0:1, b, 0:1], min_val=0, max_val=E - 1)

            def select_down(b, e):
                if b == 0:
                    act.wait_ge(q["dw_lo"], 1)
                    act.wait_ge(q["bd_ok"], 32)
                if b >= 2:
                    act.wait_ge(q["h_ready"], b - 1)
                src = raw(dws[:, bass.ds(e, 1), :, :, :]).rearrange("p e h k (a r) -> p (e h k) a r", a=1)
                dst = dsel[:, b % 2, :, :, :, :].rearrange("p h k a r -> p (h k) a r")
                a.activation(dst, src.broadcast_to((P, 2 * KD, 2, R)), ACT.Copy).then_inc(q["dsel_ok"], 1)

            def relu(b, e):
                act.wait_ge(q["h_ready"], b + 1)
                if b >= 2:
                    act.wait_ge(q["h_lo"], b - 1)
                    act.wait_ge(q["y_ready"], b - 1)
                bias = bd_sb[:, bass.ds(e, 1)]
                a.activation(ha[:, b % 2, :], h_ps[b], ACT.Relu, bias=bias).then_inc(q["h_hi"], 1)
                a.activation(h_f[R:2 * R, b % 2, :], h_ps[b][R:2 * R, :], ACT.Relu,
                             bias=bd_sb[R:2 * R, bass.ds(e, 1)]).then_inc(q["relu_ok"], 1)
                a.activation(hb[0:R, b % 2, :], h_ps[b][0:R, :], ACT.Relu,
                             bias=bd_sb[0:R, bass.ds(e, 1)]).then_inc(q["hb_ok"], 1)

            def z_hi(b):
                if b >= 2:
                    act.wait_ge(q["h_ready"], b - 1)
                for k in range(KD):
                    src = z_ps_last[k] if b == B - 1 else z_ps[:, k, :]
                    act.wait_ge(q["z_ready"], b + 1 + k if b == B - 1 else b + 1)
                    a.activation(zs[:, b % 2, HI, k, :], src, ACT.Copy,
                                 accum_out=pooled[:, b, k:k + 1]).then_inc(q["z_hi"], 1)

            def z_squares(b):
                for k in range(KD):
                    src = z_ps_last[k] if b == B - 1 else z_ps[:, k, :]
                    act.wait_ge(q["z_lo"], b + 1 + k if b == B - 1 else b + 1)
                    if b + k >= 1:
                        act.wait_ge(q["z_sq"], KD * b + k)
                    a.activation(sq[:, :], src, ACT.Square,
                                 accum_out=pooled[:, b, KD + k:KD + k + 1]).then_inc(q["z_sq"], 1)

            def u_hi(j):
                act.wait_ge(q["u_sum"], j + 1)
                copy_hi(ua[0:R + 1, 2 * j:2 * j + 2, :], u_f[0:R + 1, j % 2, :, :], q["u_hi"])

            for k in range(KD):
                act.dma_start(wkT_sb[:, k, :], wkT[k * P:(k + 1) * P, :]).then_inc(wk_in[k], 16)
            c_hi(0)
            act.wait_ge(wv_in, 16)
            copy_hi(wvs[HI][:, :, :], wv_sb[:, :, :], q["wv_hi"])
            x_hi(0)
            act.wait_ge(q["mc_ready"], 1)
            copy_hi(mc[HI][:, :, :], t_ps, q["mc_hi"])
            c_hi(1)
            v_hi(0)
            x_hi(1)
            t_hi(0)
            v_hi(1)
            exps(0)
            for i in range(0, B - 1):
                if i >= 2:
                    e = chosen(i - 2)
                    select_down(i - 2, e)
                if 2 <= i and i + 2 < B:
                    x_hi(i + 2)
                pt_hi(i)
                t_hi(i + 1)
                if i >= 1:
                    z_hi(i - 1)
                if i < 2:
                    x_hi(i + 2)
                if i == 1:
                    act.wait_ge(down_in, 16)
                    copy_hi(dws[:, :, HI, :, :], dw_sb[:, :, :, :], q["dw_hi"])
                if i >= 2:
                    relu(i - 2, e)
                if i >= 1:
                    z_squares(i - 1)
                if i == 2:
                    u_hi(2)
                    u_hi(3)
                if i + 2 < B:
                    c_hi(i + 2)
                if i >= 1:
                    v_hi(i + 1)
                if i == 0:
                    act.wait_ge(wb_in, 16)
                    copy_hi(wbs[HI][:, :, :], wb_sb[:, :, :], q["wb_hi"])
                    u_hi(0)
                exps(i + 1)
                if i == 0:
                    u_hi(1)
            L = B - 1
            e = chosen(L - 2)
            select_down(L - 2, e)
            pt_hi(L)
            relu(L - 2, e)
            z_hi(L - 1)
            z_squares(L - 1)
            z_hi(L)
            z_squares(L)
            e = chosen(L - 1)
            select_down(L - 1, e)
            e_last = chosen(L)
            select_down(L, e_last)
            relu(L - 1, e)
            relu(L, e_last)

        @block.vector
        def _(dve):
            v = nc.vector

            def sub_lo(lo, src, hi, done):
                v.tensor_tensor(lo, src, raw(hi), ALU.subtract).then_inc(done, 1)

            def moments(src, stats, mom, b, st_ok, mom_ok):
                for t in range(QT):
                    v.bn_stats(stats[:, b % 2, t, :], src[:, b, t, :]).then_inc(st_ok, 1)
                for t in range(QT):
                    dve.wait_ge(st_ok, QT * b + t + 1)
                    v.bn_aggr(mom[:, b, t, :], stats[:, b % 2, t, :]).then_inc(mom_ok, 1)

            def moments1(b):
                dve.wait_ge(x_in[b], 16)
                if b >= 2:
                    dve.wait_ge(q["mom1_ok"], QT * (b - 1))
                moments(x_sb, stats1, mom1, b, q["st1_ok"], q["mom1_ok"])

            def argmin(b):
                dve.wait_ge(q["l_ready"], b + 1)
                v.tensor_tensor(nloss[:, b, :], l_ps[b], loss_c[:, :], ALU.add).then_inc(q["nloss_ok"], 1)
                dve.wait_ge(q["nloss_ok"], b + 1)
                v.max(best[:, b, :], nloss[:, b, :]).then_inc(q["best_ok"], 1)
                dve.wait_ge(q["best_ok"], b + 1)
                v.max_index(pick[:, b, :], best[:, b, :], nloss[:, b, :]).then_inc(q["pick_ok"], 1)

            def row_max(b):
                dve.wait_ge(q["s_ready"], b + 1)
                v.reduce_max(rmax[:, b, 0:1], ps_s[:, 0:P], AX.X).then_inc(q["max_ok"], 1)
                v.reduce_max(rmax[:, b, 1:2], ps_s[:, P:SC], AX.X).then_inc(q["max_ok"], 1)
                dve.wait_ge(q["max_ok"], QT * (b + 1))
                dve.wait_ge(q["rs1_ok"], b + 1)
                v.scalar_tensor_tensor(out=nmax[:, b, :], in0=rmax[:, b, :], scalar=-1.0, in1=rs1[:, b, :],
                                       op0=ALU.mult, op1=ALU.mult).then_inc(q["nmax_ok"], 1)

            def normalize_last():
                b = B - 1
                dve.wait_ge(q["rs2_ok"], b + 1)
                dve.wait_ge(q["z_ready"], b)
                for t in range(QT):
                    v.tensor_scalar(z[:, t, :], x2[:, b, t, :], mom2[:, b, t, 0:1], rs2[:, b, t:t + 1],
                                    ALU.subtract, ALU.mult).then_inc(q["z_ok"], 1)

            def c_lo(b):
                dve.wait_ge(q["c_hi"], b + 1)
                sub_lo(cs[:, b % 2, LO, :, :], cT_sb[:, b, :, :], cs[:, b % 2, HI, :, :], q["c_lo"])

            def t_lo(b):
                dve.wait_ge(q["t_hi"], b + 1)
                sub_lo(ts[:, LO, :, :], t_ps, ts[:, HI, :, :], q["t_lo"])

            def v_lo(b):
                dve.wait_ge(q["v_hi"], b + 1)
                sub_lo(vs[:, b % 2, LO, :, :], v_ps, vs[:, b % 2, HI, :, :], q["v_lo"])

            def pt_lo(b):
                dve.wait_ge(q["pt_hi"], b + 1)
                sub_lo(pts[:, LO, :], ps_s[:, 0:SC], pts[:, HI, :], q["pt_lo"])

            def z_lo(b):
                if b < B - 1:
                    dve.wait_ge(q["z_hi"], KD * (b + 1))
                    sub_lo(zs[:, b % 2, LO, :, :], z_ps, zs[:, b % 2, HI, :, :], q["z_lo"])
                else:
                    for k in range(KD):
                        dve.wait_ge(q["z_hi"], KD * b + k + 1)
                        sub_lo(zs[:, b % 2, LO, k, :], z_ps_last[k], zs[:, b % 2, HI, k, :], q["z_lo"])

            def h_lo(b):
                dve.wait_ge(q["relu_ok"], b + 1)
                dve.wait_ge(q["h_hi"], b + 1)
                sub_lo(ha[R:2 * R, b % 2, :], h_f[R:2 * R, b % 2, :], ha[R:2 * R, b % 2, :], q["h_lo"])

            def residual(b):
                dve.wait_ge(q["exp_ok"], QT * (b + 1))
                v.reciprocal(rinv[:, b, :], rsum[:, b, :]).then_inc(q["rinv_ok"], 1)
                dve.wait_ge(q["rinv_ok"], b + 1)
                for t in range(QT):
                    dve.wait_ge(q["o_ready"], b + 1 if b < B - 1 else b + 1 + t)
                    v.scalar_tensor_tensor(out=x2[:, b, t, :], in0=o_ps[b][t], scalar=rinv[:, b, t:t + 1],
                                           in1=x_sb[:, b, t, :], op0=ALU.mult, op1=ALU.add).then_inc(q["x2_ok"], 1)

            def moments2(b):
                dve.wait_ge(q["x2_ok"], QT * (b + 1))
                if b >= 2:
                    dve.wait_ge(q["mom2_ok"], QT * (b - 1))
                moments(x2, stats2, mom2, b, q["st2_ok"], q["mom2_ok"])

            def finish(b):
                dve.wait_ge(q["y_ready"], b + 1)
                dve.wait_ge(q["z_ok"], QT * (b + 1))
                y = (ps_v if b == B - 2 else ps_y[b % 2])[:, :].rearrange("p (t d) -> p t d", t=QT)
                v.tensor_tensor(x2[:, b, :, :], y, x2[:, b, :, :], ALU.add).then_inc(q["fin_ok"], 1)

            def finish_last():
                b = B - 1
                for t in range(QT):
                    dve.wait_ge(q["y_ready"], b + 1 + t)
                    v.tensor_tensor(x2[:, b, t, :], y_ps[b][t], x2[:, b, t, :], ALU.add).then_inc(q["fin_ok"], 1)

            def fold_sum(j):
                dve.wait_ge(q["u_ready"], j + 1)
                if j >= 2:
                    dve.wait_ge(q["u_lo"], j - 1)
                bank = fold_bank[j][0:R + 1, :].rearrange("p (e d) -> p e d", e=2)
                v.tensor_tensor(u_f[0:R + 1, j % 2, :, :], bank, row_bias[0:R + 1, 2 * j:2 * j + 2, :], ALU.add).then_inc(q["u_sum"], 1)

            def fold_lo(j):
                dve.wait_ge(q["u_hi"], j + 1)
                sub_lo(ub[0:R + 1, 2 * j:2 * j + 2, :], u_f[0:R + 1, j % 2, :, :], ua[0:R + 1, 2 * j:2 * j + 2, :], q["u_lo"])

            def discriminator():
                dve.wait_ge(disc_in, 32)
                v.tensor_tensor(sg2[:, :, :], sg_sb[:, :, :], sg_sb[:, :, :], ALU.mult).then_inc(q["sg2_ok"], 1)
                dve.wait_ge(q["sg2_ok"], 1)
                v.reciprocal(inv_var[:, :, :], sg2[:, :, :]).then_inc(q["iv_ok"], 1)
                dve.wait_ge(q["iv_ok"], 1)
                v.tensor_tensor(mu_iv[:, :, :], mu_sb[:, :, :], inv_var[:, :, :], ALU.mult).then_inc(q["muiv_ok"], 1)
                dve.wait_ge(q["muiv_ok"], 1)
                v.tensor_scalar(tab_m2[:, :, :], inv_var[:, :, :], -1.0 / S, None, ALU.mult).then_inc(q["tab_ok"], 1)
                v.tensor_scalar(tab_m1[:, :, :], mu_iv[:, :, :], 2.0 / S, None, ALU.mult).then_inc(q["tab_ok"], 1)
                v.scalar_tensor_tensor(out=tab_c[:, :, :], in0=mu_iv[:, :, :], scalar=-1.0, in1=mu_sb[:, :, :],
                                       op0=ALU.mult, op1=ALU.mult).then_inc(q["tab_ok"], 1)

            v.memset(ones_col[:, :], 1.0).then_inc(q["ones_ok"], 1)
            v.memset(warm[:, :], 0.0).then_inc(q["warm_ok"], 1)
            v.memset(raw(hb[R:R + 2, :, :]), 1.0).then_inc(q["hone_ok"], 1)
            for k in range(KD):
                dve.wait_ge(wq_in[k], 16)
                v.reduce_sum(wq_sum[:, k:k + 1], wqT_sb[:, k, :], AX.X).then_inc(q["wq_summed"], 1)
                dve.wait_ge(q["wq_summed"], k + 1)
                v.tensor_scalar(wq_sum[:, k:k + 1], wq_sum[:, k:k + 1], 1.0 / D, None, ALU.mult).then_inc(q["wq_meaned"], 1)
                dve.wait_ge(q["wq_meaned"], k + 1)
                v.tensor_scalar(wqc[:, k, :], wqT_sb[:, k, :], wq_sum[:, k:k + 1], None,
                                ALU.subtract).then_inc(q["wqc_ok"], 1)

            c_lo(0)
            dve.wait_ge(q["wv_hi"], 1)
            sub_lo(wvs[LO][:, :, :], wv_sb[:, :, :], wvs[HI][:, :, :], q["wv_lo"])
            dve.wait_ge(q["x_hi"], 1)
            sub_lo(xs[:, 0, LO, :, :], xT_sb[:, 0, :, :], xs[:, 0, HI, :, :], q["x_lo"])
            dve.wait_ge(q["mc_hi"], 1)
            sub_lo(mc[LO][:, :, :], t_ps, mc[HI][:, :, :], q["mc_lo"])
            c_lo(1)
            v_lo(0)
            moments1(0)
            t_lo(0)
            moments1(1)
            row_max(0)
            v_lo(1)
            for i in range(0, B - 1):
                if i >= 4:
                    finish(i - 4)
                pt_lo(i)
                t_lo(i + 1)
                if i == 0:
                    discriminator()
                    fold_sum(0)
                if i >= 1:
                    z_lo(i - 1)
                residual(i)
                if i < B - 2:
                    moments2(i)
                row_max(i + 1)
                if i == 0:
                    dve.wait_ge(q["lossc_ready"], 1)
                    v.tensor_copy(loss_c[:, :], ps_z[0:1, 0:E]).then_inc(q["lossc_ok"], 1)
                    dve.wait_ge(q["lossc_ok"], 1)
                    fold_lo(0)
                    fold_sum(1)
                    moments1(2)
                    fold_lo(1)
                else:
                    argmin(i - 1)
                    if i == 1:
                        dve.wait_ge(q["dw_hi"], 1)
                        sub_lo(dws[:, :, LO, :, :], dw_sb[:, :, :, :], dws[:, :, HI, :, :], q["dw_lo"])
                        fold_sum(2)
                        fold_sum(3)
                    if i == 2:
                        fold_lo(2)
                        fold_lo(3)
                    if i < B - 2:
                        v_lo(i + 1)
                if i >= 2:
                    h_lo(i - 2)
                if 1 <= i and i + 2 < B:
                    moments1(i + 2)
            L = B - 1
            moments2(L - 1)
            v_lo(L)
            pt_lo(L)
            finish(L - 4)
            residual(L)
            moments2(L)
            h_lo(L - 2)
            z_lo(L - 1)
            normalize_last()
            finish(L - 3)
            finish(L - 2)
            z_lo(L)
            argmin(L - 1)
            argmin(L)
            h_lo(L - 1)
            h_lo(L)
            finish(L - 1)
            finish_last()

        @block.tensor
        def _(pe):
            t = nc.tensor

            def mm(dst, lhsT, rhs, start, stop):
                return t.matmul(dst, lhsT, rhs, start=start, stop=stop, skip_group_check=True)

            def mm_split(dst, lhs, rhs, start, stop):
                mm(dst, lhs[LO], rhs[HI], start, False)
                mm(dst, lhs[HI], rhs[LO], False, False)
                return mm(dst, lhs[HI], rhs[HI], False, stop)

            def project_t(b):
                pe.wait_ge(q["x_lo"], b + 1)
                if b == 0:
                    pe.wait_ge(q["mc_lo"], 1)
                else:
                    pe.wait_ge(q["t_lo"], b)
                for m in range(KD):
                    for k in range(KD):
                        last = mm_split(t_ps[:, m, :], [mc[h][:, k, m * P:(m + 1) * P] for h in (HI, LO)],
                                        [xs[:, b % 2, h, k, :] for h in (HI, LO)], k == 0, k == KD - 1)
                last.then_inc(q["t_ready"], 1)

            def project_v(b):
                pe.wait_ge(q["c_lo"], b + 1)
                if b == 0:
                    pe.wait_ge(q["wv_lo"], 1)
                else:
                    pe.wait_ge(q["v_lo"], b)
                for m in range(QT):
                    for k in range(KD):
                        last = mm_split(v_ps[:, m, :], [cs[:, b % 2, h, k, m * P:(m + 1) * P] for h in (HI, LO)],
                                        [wvs[h][:, k, :] for h in (HI, LO)], k == 0, k == KD - 1)
                last.then_inc(q["v_ready"], 1)

            def scores(b):
                pe.wait_ge(q["t_lo"], b + 1)
                pe.wait_ge(q["c_lo"], b + 1)
                if b == 0:
                    pe.wait_ge(q["idh_ok"], 1)
                    pe.wait_ge(q["mask_ok"], 1)
                else:
                    pe.wait_ge(q["pt_lo"], b)
                for m in range(QT):
                    lo = 0 if m == 0 else P
                    keys = (m + 1) * P
                    dst = ps_s[:, lo:lo + keys]
                    for k in range(KD):
                        mm_split(dst, [ts[:, h, k, m * P:(m + 1) * P] for h in (HI, LO)],
                                 [cs[:, b % 2, h, k, 0:keys] for h in (HI, LO)], k == 0, False)
                    last = mm(ps_s[:, lo + keys - P:lo + keys], ident_h[:, :], mask_h[:, :], False, True)
                last.then_inc(q["s_ready"], 1)

            def transpose_p(b):
                pe.wait_ge(q["exp_ok"], QT * (b + 1))
                if b == 0:
                    pe.wait_ge(q["id_ok"], 1)
                for j in range(SC // P):
                    last = t.transpose(ps_s[:, j * P:(j + 1) * P], prob[:, j * P:(j + 1) * P], ident[:, :])
                last.then_inc(q["pt_ready"], 1)

            def attend(b):
                pe.wait_ge(q["pt_lo"], b + 1)
                pe.wait_ge(q["v_lo"], b + 1)
                if b >= 1:
                    pe.wait_ge(q["x2_ok"], QT * b)
                for m, j, k, first, stop in ((0, 0, 0, True, True), (1, 1, 0, True, False), (1, 2, 1, False, True)):
                    last = mm_split(o_ps[b][m], [pts[:, h, j * P:(j + 1) * P] for h in (HI, LO)],
                                    [vs[:, b % 2, h, k, :] for h in (HI, LO)], first, stop)
                    if b == B - 1 and stop:
                        last.then_inc(q["o_ready"], 1)
                if b < B - 1:
                    last.then_inc(q["o_ready"], 1)

            def transpose_z(b):
                pe.wait_ge(q["z_ok"], QT * (b + 1))
                if b == 0:
                    pe.wait_ge(q["lossc_ok"], 1)
                else:
                    pe.wait_ge(q["z_sq"], KD * b)
                for k in range(KD):
                    dst = z_ps_last[k] if b == B - 1 else z_ps[:, k, :]
                    for m in range(QT):
                        last = t.transpose(dst[:, m * P:(m + 1) * P], z[:, m, k * P:(k + 1) * P], ident[:, :])
                    if b == B - 1 or k == KD - 1:
                        last.then_inc(q["z_ready"], 1)

            def base(b, tiles=range(QT)):
                pe.wait_ge(q["z_lo"], b + 1 if b < B - 1 else B - 1 + KD)
                if b == 0:
                    pe.wait_ge(q["wb_lo"], 1)
                if b < 2:
                    pe.wait_ge(q["u_sum"], b + 3)
                elif b == B - 2:
                    pe.wait_ge(q["x2_ok"], QT * B)
                else:
                    pe.wait_ge(q["fin_ok"], b - 1)
                for m in tiles:
                    for k in range(KD):
                        mm_split(y_ps[b][m],
                                 [zs[:, b % 2, h, k, m * P:(m + 1) * P] for h in (HI, LO)],
                                 [wbs[h][:, k, :] for h in (HI, LO)], k == 0 and (m == 0 or b == B - 1), False)

            def loss_constant():
                pe.wait_ge(q["tab_ok"], 3)
                pe.wait_ge(q["ones_ok"], 1)
                for k in range(KD):
                    last = mm(ps_z[0:1, 0:E], ones_col[:, :], tab_c[:, k, :], k == 0, k == KD - 1)
                last.then_inc(q["lossc_ready"], 1)

            def losses(b):
                pe.wait_ge(q["z_sq"], KD * (b + 1))
                if b == 0:
                    pe.wait_ge(q["u_sum"], 1)
                elif b < B - 1:
                    pe.wait_ge(q["nloss_ok"], b)
                    pe.wait_ge(q["hb_ok"], b)
                tabs = [tab_m1, tab_m2]
                for j in range(2 * KD):
                    last = mm(l_ps[b], pooled[:, b, j:j + 1], tabs[j // KD][:, j % KD, :], j == 0, j == 2 * KD - 1)
                last.then_inc(q["l_ready"], 1)

            def down(b):
                pe.wait_ge(q["dsel_ok"], b + 1)
                pe.wait_ge(q["nloss_ok"], b + 1)
                if b == B - 1:
                    pe.wait_ge(q["z_sq"], KD * B)
                for k in range(KD):
                    last = mm_split(h_ps[b], [dsel[:, b % 2, h, k, :, :].rearrange("p a r -> p (a r)") for h in (HI, LO)],
                                    [zs[:, b % 2, h, k, :] for h in (HI, LO)], k == 0, k == KD - 1)
                last.then_inc(q["h_ready"], 1)

            def chosen(b):
                pe.wait_ge(q["pick_ok"], b + 1)
                return pe.value_load(pick[0:1, b, 0:1], min_val=0, max_val=E - 1)

            def expert(b, e):
                pe.wait_ge(q["hb_ok"], b + 1)
                pe.wait_ge(q["h_lo"], b + 1)
                if b == 0:
                    pe.wait_ge(q["hone_ok"], 1)
                    pe.wait_ge(q["u_twice"], 16)
                for m in range(QT):
                    mm(y_ps[b][m], hb[0:R + 2, b % 2, m * P:(m + 1) * P], ub[0:R + 2, bass.ds(e, 1), :], False, False)
                    last = mm(y_ps[b][m], ha[:, b % 2, m * P:(m + 1) * P], ua[:, bass.ds(e, 1), :],
                              False, m == QT - 1 or b == B - 1)
                    if b == B - 1 or m == QT - 1:
                        last.then_inc(q["y_ready"], 1)

            def fold(j, parts=(0, 1)):
                pe.wait_ge(up_in[j // 2], 16)
                pe.wait_ge(conv_in[j], 16)
                if j == 3:
                    pe.wait_ge(q["u_sum"], 2)
                bank = fold_bank[j]
                for s in parts:
                    for k in range(KD):
                        last = mm(bank[0:R + 1, s * D:(s + 1) * D], up_sb[:, 2 * j + s, k, :], cw_sb[:, 2 * j + s, k, :],
                                  k == 0, k == KD - 1)
                if s == 1:
                    last.then_inc(q["u_ready"], 1)

            pe.wait_ge(q["warm_ok"], 1)
            for _ in range(WARM):
                mm(ps_y[1][:, :], warm[:, 0:P], warm[:, :], True, True)
            for k in range(KD):
                pe.wait_ge(wk_in[k], 16)
                pe.wait_ge(q["wqc_ok"], k + 1)
                for m in range(KD):
                    last = mm(t_ps[:, m, :], wqc[:, k, m * P:(m + 1) * P], wkT_sb[:, k, :],
                              k == 0 and m == 0, k == KD - 1)
            last.then_inc(q["mc_ready"], 1)
            project_v(0)
            project_t(0)
            project_v(1)
            scores(0)
            for i in range(0, B - 1):
                project_t(i + 1)
                if i == 0:
                    fold(0, (0,))
                transpose_p(i)
                if i >= 1:
                    transpose_z(i - 1)
                if i >= 2:
                    down(i - 2)
                if i == 0:
                    fold(0, (1,))
                    fold(1, (0,))
                else:
                    project_v(i + 1)
                attend(i)
                scores(i + 1)
                if i == 0:
                    loss_constant()
                    fold(1, (1,))
                    fold(2)
                else:
                    losses(i - 1)
                if i == 1:
                    fold(3)
                if i >= 2:
                    base(i - 2)
                if i >= 3:
                    expert(i - 3, chosen(i - 3))
            L = B - 1
            transpose_p(L)
            down(L - 2)
            attend(L)
            base(L - 2, (0,))
            transpose_z(L - 1)
            base(L - 2, (1,))
            expert(L - 3, chosen(L - 3))
            expert(L - 2, chosen(L - 2))
            base(L - 1, (0,))
            transpose_z(L)
            losses(L - 1)
            base(L - 1, (1,))
            losses(L)
            base(L, (0,))
            down(L - 1)
            down(L)
            base(L, (1,))
            expert(L - 1, chosen(L - 1))
            expert(L, chosen(L))


_INS = ["x", "xT", "ctxT", "wqT", "wkT", "wv", "base_wT", "mu_T", "sigma_T",
        "down_w", "down_bT", "up_aug", "conv_wT", "conv_b", "base_b"]


def kernel(**inputs):
    import numpy as _np
    import concourse.bacc as _bacc
    from concourse import mybir as _mybir
    from concourse.bass_utils import run_bass_kernel_spmd as _run

    a = {n: _np.asarray(v) for n, v in inputs.items()}

    def by_partition(w):
        e, d, r = w.shape
        return w.reshape(e, d // 128, 128, r).transpose(2, 0, 1, 3)

    laid = {
        "x": a["x"],
        "xT": a["x"].transpose(0, 2, 1),
        "ctxT": a["ctx_1024"].transpose(0, 2, 1),
        "wqT": a["L0_xattn_w_q"].T,
        "wkT": a["L0_xattn_w_k"].T,
        "wv": a["L0_xattn_w_v"],
        "base_wT": a["L0_ffn_base_W"].T,
        "mu_T": a["L0_ffn_disc_mu"].T,
        "sigma_T": a["L0_ffn_disc_sigma"].T,
        "down_w": by_partition(a["L0_ffn_down_W"]),
        "down_bT": a["L0_ffn_down_b"].T,
        "up_aug": by_partition(_np.concatenate([a["L0_ffn_up_W"].transpose(0, 2, 1), a["L0_ffn_up_b"][:, :, None]], axis=2)),
        "conv_wT": a["L0_ffn_conv_W"].transpose(0, 2, 1),
        "conv_b": a["L0_ffn_conv_b"],
        "base_b": a["L0_ffn_base_b"],
    }
    nc = _bacc.Bacc("TRN2", target_bir_lowering=False, num_devices=1)
    arrays, args = {}, []
    for name in _INS:
        arr = _np.ascontiguousarray(laid[name])
        arrays[f"in_{name}"] = arr
        args.append(nc.dram_tensor(f"in_{name}", arr.shape, _mybir.dt.from_np(arr.dtype), kind="ExternalInput").ap())
    out = nc.dram_tensor("out_0", a["x"].shape, _mybir.dt.from_np(a["x"].dtype), kind="ExternalOutput").ap()
    xattn_ffn_program(nc, *args, out)
    r = _run(nc, [arrays], core_ids=[0])
    return r.results[0]["out_0"]
```
